# Optimizing a Trainium2 kernel written in Bass

```python
import numpy as np
import jax
import jax.numpy as jnp

def _softmax(x, axis=-1):
    return jax.nn.softmax(x, axis=axis)

def _gelu(x):
    return jax.nn.gelu(x, approximate=True)

def _silu(x):
    return jax.nn.silu(x)

def _sigmoid(x):
    return jax.nn.sigmoid(x)

def _layernorm(x, axis=-1, eps=1e-05):
    m = jnp.mean(x, axis=axis, keepdims=True)
    v = jnp.var(x, axis=axis, keepdims=True)
    return (x - m) / jnp.sqrt(v + eps)

def _scatter_add(tgt, idx, src, axis=0):
    return tgt.at[idx].add(src)

def _segment_sum(src, seg, n):
    return jax.ops.segment_sum(src, seg, n)
kernel_name = 'mk_seq_postln_d1_jaxref_r4_5f6fe2'

def setup_inputs(seed: int=0):
    np.random.seed(seed)
    _w = jnp.asarray

    def _L0_attn_setup():
        import jax, jax.numpy as jnp
        import numpy as np
        import math
        N_HEAD = 16
        HEAD_DIM = 64
        N_EMBD = 256
        EPS_RMS = 1e-05
        U_L2_EPS = 1e-06

        def _get_alibi_slopes(n_heads):

            def pow2(n):
                start = 2 ** (-2 ** (-(math.log2(n) - 3)))
                return [start * start ** i for i in range(n)]
            if math.log2(n_heads).is_integer():
                return pow2(n_heads)
            c = 2 ** math.floor(math.log2(n_heads))
            s = pow2(c)
            extra = _get_alibi_slopes(2 * c)
            return s + extra[0::2][:n_heads - c]

        def _rmsnorm(x, w):
            var = jnp.mean(jnp.square(x), axis=-1, keepdims=True)
            return x * jax.lax.rsqrt(var + EPS_RMS) * w
        key = jax.random.key(seed)
        ks = jax.random.split(key, 9)
        B, T = (2, 512)
        H, D, C = (N_HEAD, HEAD_DIM, N_EMBD)
        x = jax.random.normal(ks[0], (B, T, C), dtype=jnp.float32)
        sc = 1.0 / math.sqrt(C)
        Wq = jax.random.normal(ks[1], (C, H * D), dtype=jnp.float32) * sc
        Wk = jax.random.normal(ks[2], (C, H * D), dtype=jnp.float32) * sc
        Wv = jax.random.normal(ks[3], (C, H * D), dtype=jnp.float32) * sc
        Wproj = jax.random.normal(ks[4], (H * D, C), dtype=jnp.float32) * (0.5 / math.sqrt(C) / math.sqrt(12))
        q_rms_w = jnp.ones((D,), dtype=jnp.float32)
        k_rms_w = jnp.ones((D,), dtype=jnp.float32)
        omega = jnp.full((H,), math.log(math.expm1(1.0)), dtype=jnp.float32)
        u = jax.random.normal(ks[5], (H, D), dtype=jnp.float32) * (1.0 / math.sqrt(D))
        return {'x': x, 'Wq': Wq, 'Wk': Wk, 'Wv': Wv, 'Wproj': Wproj, 'q_rms_w': q_rms_w, 'k_rms_w': k_rms_w, 'omega': omega, 'u': u}
    _L0_attn_in = _L0_attn_setup()

    def _L0_ffn_setup():
        import jax, jax.numpy as jnp
        import numpy as np
        D_IN, D_HID = (256, 1024)

        def _ternary(key, shape):
            return jax.random.randint(key, shape, -1, 2).astype(jnp.float32)

        def _tlin(x, w, s):
            return jnp.einsum('bsi,oi->bso', x, w) * s
        key = jax.random.key(seed)
        ks = jax.random.split(key, 12)
        inv = lambda fan: 1.0 / np.sqrt(fan).astype(np.float32)
        return {'x': jax.random.normal(ks[0], (4, 512, D_IN), dtype=jnp.float32), 'w1_w': _ternary(ks[1], (D_HID, D_IN)), 'w1_s': jax.random.uniform(ks[2], (D_HID,), dtype=jnp.float32) * inv(D_IN), 'w2_w': _ternary(ks[3], (D_HID, D_IN)), 'w2_s': jax.random.uniform(ks[4], (D_HID,), dtype=jnp.float32) * inv(D_IN), 'h1_w': _ternary(ks[5], (D_HID, D_HID)), 'h1_s': jax.random.uniform(ks[6], (D_HID,), dtype=jnp.float32) * inv(D_HID), 'h2_w': _ternary(ks[7], (D_HID, D_HID)), 'h2_s': jax.random.uniform(ks[8], (D_HID,), dtype=jnp.float32) * inv(D_HID), 'w3_w': _ternary(ks[9], (D_IN, D_HID)), 'w3_s': jax.random.uniform(ks[10], (D_IN,), dtype=jnp.float32) * inv(D_HID)}
    _L0_ffn_in = _L0_ffn_setup()
    _d = {'L0_attn_x': _L0_attn_in['x'], 'L0_attn_Wq': _L0_attn_in['Wq'], 'L0_attn_Wk': _L0_attn_in['Wk'], 'L0_attn_Wv': _L0_attn_in['Wv'], 'L0_attn_Wproj': _L0_attn_in['Wproj'], 'L0_attn_q_rms_w': _L0_attn_in['q_rms_w'], 'L0_attn_k_rms_w': _L0_attn_in['k_rms_w'], 'L0_attn_omega': _L0_attn_in['omega'], 'L0_attn_u': _L0_attn_in['u'], 'L0_ffn_w1_w': _L0_ffn_in['w1_w'], 'L0_ffn_w1_s': _L0_ffn_in['w1_s'], 'L0_ffn_w2_w': _L0_ffn_in['w2_w'], 'L0_ffn_w2_s': _L0_ffn_in['w2_s'], 'L0_ffn_h1_w': _L0_ffn_in['h1_w'], 'L0_ffn_h1_s': _L0_ffn_in['h1_s'], 'L0_ffn_h2_w': _L0_ffn_in['h2_w'], 'L0_ffn_h2_s': _L0_ffn_in['h2_s'], 'L0_ffn_w3_w': _L0_ffn_in['w3_w'], 'L0_ffn_w3_s': _L0_ffn_in['w3_s']}
    _x0 = _d['L0_attn_x']
    _d['L0_attn_x'] = jax.random.normal(jax.random.fold_in(jax.random.key(seed), 1), (2, 2048, 256), dtype=_x0.dtype)
    del _x0
    return _d

def reference(L0_attn_x, L0_attn_Wq, L0_attn_Wk, L0_attn_Wv, L0_attn_Wproj, L0_attn_q_rms_w, L0_attn_k_rms_w, L0_attn_omega, L0_attn_u, L0_ffn_w1_w, L0_ffn_w1_s, L0_ffn_w2_w, L0_ffn_w2_s, L0_ffn_h1_w, L0_ffn_h1_s, L0_ffn_h2_w, L0_ffn_h2_s, L0_ffn_w3_w, L0_ffn_w3_s):

    def _L0_attn_ref(x, Wq, Wk, Wv, Wproj, q_rms_w, k_rms_w, omega, u):
        import jax, jax.numpy as jnp
        import numpy as np
        import math
        N_HEAD = 16
        HEAD_DIM = 64
        N_EMBD = 256
        EPS_RMS = 1e-05
        U_L2_EPS = 1e-06

        def _get_alibi_slopes(n_heads):

            def pow2(n):
                start = 2 ** (-2 ** (-(math.log2(n) - 3)))
                return [start * start ** i for i in range(n)]
            if math.log2(n_heads).is_integer():
                return pow2(n_heads)
            c = 2 ** math.floor(math.log2(n_heads))
            s = pow2(c)
            extra = _get_alibi_slopes(2 * c)
            return s + extra[0::2][:n_heads - c]

        def _rmsnorm(x, w):
            var = jnp.mean(jnp.square(x), axis=-1, keepdims=True)
            return x * jax.lax.rsqrt(var + EPS_RMS) * w
        B, T, C = x.shape
        H, D = (N_HEAD, HEAD_DIM)
        q = (x @ Wq).reshape(B, T, H, D)
        k = (x @ Wk).reshape(B, T, H, D)
        v = (x @ Wv).reshape(B, T, H, D)
        q = _rmsnorm(q, q_rms_w)
        k = _rmsnorm(k, k_rms_w)
        slopes = jnp.asarray(_get_alibi_slopes(H), dtype=jnp.float32)
        omega_eff = jax.nn.softplus(omega) * slopes
        u_n = u / jnp.maximum(jnp.linalg.norm(u, axis=-1, keepdims=True), U_L2_EPS)
        gate_logits = jnp.einsum('bthd,hd->bht', k, u_n) / math.sqrt(D)
        gate = jax.nn.softplus(gate_logits)
        idx = jnp.arange(T)
        dist = jnp.maximum(idx[:, None] - idx[None, :], 0).astype(jnp.float32)
        bias = -dist[None, None] * omega_eff[None, :, None, None] * gate[:, :, None, :]
        causal = idx[:, None] >= idx[None, :]
        bias = jnp.where(causal[None, None], bias, -jnp.inf)
        scale = 1.0 / math.sqrt(D)
        scores = jnp.einsum('bihd,bjhd->bhij', q, k) * scale + bias
        attn = jax.nn.softmax(scores, axis=-1)
        y = jnp.einsum('bhij,bjhd->bihd', attn, v).reshape(B, T, H * D)
        return y @ Wproj

    def _L0_ffn_ref(x, w1_w, w1_s, w2_w, w2_s, h1_w, h1_s, h2_w, h2_s, w3_w, w3_s):
        import jax, jax.numpy as jnp
        import numpy as np
        D_IN, D_HID = (256, 1024)

        def _ternary(key, shape):
            return jax.random.randint(key, shape, -1, 2).astype(jnp.float32)

        def _tlin(x, w, s):
            return jnp.einsum('bsi,oi->bso', x, w) * s
        h = jax.nn.silu(_tlin(x, w1_w, w1_s)) * _tlin(x, w2_w, w2_s)
        h = jax.nn.gelu(_tlin(h, h1_w, h1_s), approximate=False)
        h = jax.nn.gelu(_tlin(h, h2_w, h2_s), approximate=False)
        return _tlin(h, w3_w, w3_s)
    x = L0_attn_x
    x = _layernorm(x + _L0_attn_ref(x, L0_attn_Wq, L0_attn_Wk, L0_attn_Wv, L0_attn_Wproj, L0_attn_q_rms_w, L0_attn_k_rms_w, L0_attn_omega, L0_attn_u), axis=-1)
    x = _layernorm(x + _L0_ffn_ref(x, L0_ffn_w1_w, L0_ffn_w1_s, L0_ffn_w2_w, L0_ffn_w2_s, L0_ffn_h1_w, L0_ffn_h1_s, L0_ffn_h2_w, L0_ffn_h2_s, L0_ffn_w3_w, L0_ffn_w3_s), axis=-1)
    return x

_drawn_inputs = setup_inputs


def setup_inputs(seed=0):
    import zlib

    import numpy as np

    out = dict(_drawn_inputs(seed))
    spreads = {'L0_attn_q_rms_w': (1.0, 0.6),
     'L0_attn_k_rms_w': (1.0, 0.6),
     'L0_attn_omega': (0.5413248538970947, 0.6)}
    factors = {'L0_attn_u': 8.0,
     'L0_ffn_w1_w': 8.0,
     'L0_ffn_w1_s': 8.0,
     'L0_ffn_w2_w': 8.0,
     'L0_ffn_w2_s': 8.0,
     'L0_ffn_h1_w': 8.0,
     'L0_ffn_h1_s': 8.0,
     'L0_ffn_h2_w': 8.0,
     'L0_ffn_h2_s': 8.0,
     'L0_ffn_w3_w': 8.0,
     'L0_ffn_w3_s': 8.0}
    for name, (base, spread) in spreads.items():
        noise = np.random.default_rng([zlib.crc32(name.encode()), seed]).standard_normal(out[name].shape)
        drawn = base * np.exp(spread * noise) if base else spread * noise
        out[name] = jnp.asarray(drawn.astype(out[name].dtype))
    for name, factor in factors.items():
        out[name] = (out[name] * factor).astype(out[name].dtype)
    return out
```

```python
import concourse.bass as bass
from concourse import mybir
from contextlib import ExitStack

F32 = mybir.dt.float32
F32R = mybir.dt.float32r
ACT = mybir.ActivationFunctionType
ALU = mybir.AluOpType
AX = mybir.AxisListType

B, T, C = 2, 2048, 256
H, D = 16, 64
HID = 1024
P = 128
TT = T // P
KC = C // P
QB = 512
NQB = T // QB
TQ = QB // P
NEG = -1.0e30
EPS_RMS, EPS_U, EPS_LN = 1e-5, 1e-6, 1e-5

CQ, CK, CG, CV = 0, D, 2 * D, 2 * D + 1
WCOLS = 3 * D + 2
ONE = WCOLS - 1
R_BIAS, R_SHIFT = D, 96

UNITS = [(qb, kt) for qb in range(NQB) for kt in range(TQ * (qb + 1))]
MAXES = [(qt, kc) for qt in range(TT) for kc in range(qt // TQ + 1)]
NU, NM = len(UNITS), len(MAXES)
LAG = 2
PR = 4
NPJ = TT // 2
NTR = 2 * NQB + NQB
NYM = 3
NXT = TT // 2
YMB = NXT + (H // 2) * NQB * NYM
GATE = 24
BEFORE = 2 * NU
GP_CONSTANTS = 22 + H


def group_end(qb):
    return sum(1 for qt, _ in MAXES if qt // TQ <= qb)


def segment_steps(main, prep, second):
    steps = []
    prep_at = {}
    if prep:
        for j in range(NPJ):
            prep_at.setdefault(j, []).append(("project", j))
        prep_at.setdefault(8, []).append(("square",))
        prep_at.setdefault(11, []).append(("sumsq",))
        prep_at.setdefault(17, []).append(("normalise",))
        for i in range(2 * NQB):
            prep_at.setdefault(19 + i, []).append(("turn", i))
        v = 0
        first, last = 22, NU - 1
        for qb in range(NQB):
            n = group_end(qb) - v
            for w in range(n):
                at = first + (v + w) * (last - first) // (NM - 1)
                at = max(at, 19 + 2 * qb + 2)
                prep_at.setdefault(at, []).append(("max", v + w))
            v += n
            prep_at.setdefault(at, []).append(("negmax", qb))
            prep_at.setdefault(min(max(at + 1, 19 + 2 * NQB), NU + 1), []).append(("shift", qb))
    for u in range(NU + LAG + 1):
        if main and u < NU:
            steps.append(("scores", u))
        if main and LAG <= u < NU + LAG:
            steps.append(("values", u - LAG))
            qb, kt = UNITS[u - LAG]
            if kt == TQ * (qb + 1) - 1:
                steps.append(("divide", qb))
                if second:
                    for i in range(NYM):
                        prep_at.setdefault(min(u + 1 + i, NU + LAG), []).append(("out", qb, i))
        if main or prep:
            steps.extend(prep_at.get(u, []))
    return steps


def attention(nc, x, wq, wk, wv, wproj, q_rms_w, k_rms_w, omega, u, x1_dram):
    ctx = ExitStack()
    with ctx:
        def sb(name, shape, dt=F32):
            return ctx.enter_context(nc.sbuf_tensor(name, shape, dt))

        def pb(name):
            return ctx.enter_context(nc.psum_tensor(name, [P, 512], F32))

        def sem(name):
            return ctx.enter_context(nc.semaphore(name))

        ident = sb("ident", [P, P])
        ident_r = sb("ident_r", [P, P], F32R)
        mask_kq = sb("mask_kq", [P, P], F32R)
        mask_qk = sb("mask_qk", [P, P], F32R)
        mask_f = sb("mask_f", [P, 2, P])
        acc = sb("acc", [P, TT, C])
        xt_hi = sb("xt_hi", [P, KC, T], F32R)
        xt_lo = sb("xt_lo", [P, KC, T], F32R)
        w_in = sb("w_in", [P, KC, WCOLS])
        w_hi = sb("w_hi", [P, KC, WCOLS], F32R)
        w_lo = sb("w_lo", [P, KC, WCOLS], F32R)
        wg_tmp = sb("wg_tmp", [P, KC, D])
        raw = [sb(f"raw{i}", [P, TT, WCOLS]) for i in range(2)]
        k_tok = sb("k_tok", [P, TT, P])
        q_tok = sb("q_tok", [P, TT, P])
        k_split = [sb(f"k_split{i}", [P, T], F32R) for i in range(2)]
        q_twice = [sb(f"q_twice{i}", [P, T], F32R) for i in range(2)]
        k_ext = [sb(f"k_ext{i}", [P, T], F32R) for i in range(2)]
        q_ext = [sb(f"q_ext{i}", [P, T], F32R) for i in range(2)]
        q_max = [sb(f"q_max{i}", [P, T], F32R) for i in range(2)]
        bias = [sb(f"bias{i}", [P, TT, NQB]) for i in range(2)]
        away = sb("away", [P, TT, NQB])
        key_no = sb("key_no", [P, TT])
        exps = sb("exps", [P, PR, QB])
        y_tok = sb("y_tok", [P, TT, P])
        yt_hi = sb("yt_hi", [P, QB], F32R)
        yt_lo = sb("yt_lo", [P, QB], F32R)
        wp_in = sb("wp_in", [P, C])
        wp_hi = sb("wp_hi", [P, C], F32R)
        wp_lo = sb("wp_lo", [P, C], F32R)
        sumsq = sb("sumsq", [P, 2, TT])
        mean_sq = sb("mean_sq", [P, 2, TT])
        rs = sb("rs", [P, 2, TT])
        power = sb("power", [P, 2 * TT])
        g = sb("g", [P, 10, TT])
        c_hi = sb("c_hi", [P, TT], F32R)
        jc_hi = sb("jc_hi", [P, TT], F32R)
        maxes = sb("maxes", [P, TT, NQB])
        neg_max = sb("neg_max", [P, TT], F32R)
        recip = sb("recip", [P, TQ])
        stats = sb("stats", [P, TT, 6])
        mean_var = sb("mean_var", [P, TT, 2])
        ln_rs = sb("ln_rs", [P, TT])
        omega_eff = sb("omega_eff", [P, H])
        slopes = sb("slopes", [P, H])
        u_gate = sb("u_gate", [P, H, D])
        u_norm = sb("u_norm", [P, 2, H])
        half = sb("half", [P, H])
        one = sb("one", [P, KC])
        qk_w = sb("qk_w", [P, D])
        rms_in = sb("rms_in", [P, 2, D])

        ps_s = [pb(f"ps_s{i}") for i in range(2)]
        ps_m = [pb(f"ps_m{i}") for i in range(2)]
        ps_v = pb("ps_v")
        ps_p = pb("ps_p")
        ps_t = pb("ps_t")
        ps_y = pb("ps_y")

        s_par = sem("s_par")
        s_cg = sem("s_cg")
        s_cv = sem("s_cv")
        s_ce = sem("s_ce")
        s_pw = sem("s_pw")
        s_const = sem("s_const")
        x_in = sem("x_in")
        w_load = sem("w_load")
        wg_t = sem("wg_t")
        wg_done = sem("wg_done")
        w_done = sem("w_done")
        wp_load = sem("wp_load")
        wp_done = sem("wp_done")
        pj_full = sem("pj_full")
        pj_free = sem("pj_free")
        sq_done = sem("sq_done")
        ss_part = sem("ss_part")
        ms_done = sem("ms_done")
        rs_done = sem("rs_done")
        nrm = sem("nrm")
        gate = sem("gate")
        gate_e = sem("gate_e")
        tok_done = sem("tok_done")
        tr_full = sem("tr_full")
        tr_free = sem("tr_free")
        qk_hi = sem("qk_hi")
        dup = [sem(f"dup{i}") for i in range(NQB)]
        mx_full = sem("mx_full")
        mx_free = sem("mx_free")
        nm_done = sem("nm_done")
        st_full = sem("st_full")
        ex_done = sem("ex_done")
        pv_done = sem("pv_done")
        rc_done = sem("rc_done")
        y_done = sem("y_done")
        ym_full = sem("ym_full")
        ym_free = sem("ym_free")
        yt_done = sem("yt_done")
        bn_done = sem("bn_done")
        lnv_done = sem("lnv_done")
        lnr_done = sem("lnr_done")
        ln_done = sem("ln_done")
        x1_out = sem("x1_out")

        def over_heads(eng, segment, begin, end):
            with eng.Fori(0, B) as b:
                begin(b)
                segment(b, None, 0, 0, 0)
                with eng.Fori(0, H // 2 - 1) as hp:
                    segment(b, 2 * hp, 2 * hp + 1, 0, hp)
                    segment(b, 2 * hp + 1, 2 * hp + 2, 1, hp)
                hp = H // 2 - 1
                segment(b, 2 * hp, 2 * hp + 1, 0, hp)
                segment(b, 2 * hp + 1, None, 1, hp)
                end(b)

        def steps_of(main, prep, second):
            return segment_steps(main is not None, prep is not None, second == 1)

        block = ctx.enter_context(nc.Block())

        @block.sync
        def _(sp):
            for w, src in ((rms_in[:, 0, :], q_rms_w), (rms_in[:, 1, :], k_rms_w), (omega_eff[:], omega),
                           (u_gate[:].rearrange("p h d -> p (h d)"), u.rearrange("h d -> (h d)"))):
                sp.dma_start(w, src.partition_broadcast(P)).then_inc(s_par, 16)

            def load_weights(n, h):
                sp.wait_ge(w_done, 1 + 2 * n)
                for dst, src in ((CQ, wq), (CK, wk), (CV, wv)):
                    sp.dma_start(w_in[:, :, dst:dst + D],
                                 src[:, bass.ds(h * D, D)].rearrange("(k p) d -> p k d", p=P)).then_inc(w_load, 16)

            def begin(b):
                sp.wait_ge(x1_out, 16 * b + 1)
                sp.dma_start(acc[:], x[bass.ds(b * T, T), :].rearrange("(t p) c -> p t c", p=P)).then_inc(x_in, 16)

            def segment(b, main, prep, second, hp):
                if prep is not None:
                    n = b * H + prep
                    load_weights(n, prep)
                if second == 0 and main is not None:
                    pair = b * (H // 2) + hp
                    sp.wait_ge(wp_done, 1 + 2 * pair)
                    sp.dma_start(wp_in[:], wproj[bass.ds(hp * P, P), :]).then_inc(wp_load, 16)
                if prep is not None:
                    s = (1 - second) if main is not None else 0
                    for qc in range(NQB):
                        cols = slice(qc * QB, (qc + 1) * QB)
                        sp.wait_ge(qk_hi, 1 + 2 * NQB * n + 2 * qc + 1)
                        sp.dma_start(k_split[s][0:D, cols].bitcast(F32), k_ext[s][0:D, cols].bitcast(F32)).then_inc(dup[qc], 16)
                        sp.wait_ge(qk_hi, 1 + 2 * NQB * n + 2 * qc + 2)
                        sp.dma_start(q_twice[s][0:D, cols].bitcast(F32), q_max[s][0:D, cols].bitcast(F32)).then_inc(dup[qc], 16)
                        sp.dma_start(q_twice[s][D:P, cols].bitcast(F32), q_max[s][0:D, cols].bitcast(F32)).then_inc(dup[qc], 16)

            def end(b):
                sp.wait_ge(ln_done, b + 1)
                sp.dma_start(x1_dram[bass.ds(b * T, T), :].rearrange("(t p) c -> p t c", p=P), acc[:]).then_inc(x1_out, 16)

            sp.sem_inc(x1_out, 1)
            over_heads(sp, segment, begin, end)
            sp.wait_ge(x1_out, 16 * B + 1)

        @block.gpsimd
        def _(gp):
            made = [0]

            def link(ins):
                made[0] += 1
                ins.then_inc(s_cg, 1)
                gp.wait_ge(s_cg, made[0])

            link(nc.gpsimd.memset(ident[:], 0.0))
            link(nc.gpsimd.memset(mask_f[:], 0.0))
            link(nc.gpsimd.memset(k_tok[:], 0.0))
            link(nc.gpsimd.memset(q_tok[:], 0.0))
            link(nc.gpsimd.memset(y_tok[:], 0.0))
            link(nc.gpsimd.memset(power[:], -0.5))
            link(nc.gpsimd.memset(half[:], 0.5))
            link(nc.gpsimd.memset(one[:], 1.0))
            for i in range(2):
                link(nc.gpsimd.memset(raw[i][:, :, ONE:ONE + 1], 1.0))
            link(nc.gpsimd.memset(w_in[:, :, CG:CG + 1], 0.0))
            link(nc.gpsimd.memset(w_in[:, :, ONE:ONE + 1], 0.0))
            for h in range(H):
                link(nc.gpsimd.memset(slopes[:, h:h + 1], 2.0 ** (-0.5 * (h + 1))))
            link(nc.gpsimd.affine_select(out=ident[:], in_=ident[:], compare_op=ALU.not_equal, fill=1.0, base=0,
                                        pattern=[[-1, P]], channel_multiplier=1))
            link(nc.gpsimd.affine_select(out=mask_f[:, 0, :], in_=mask_f[:, 0, :], compare_op=ALU.is_ge, fill=NEG,
                                        base=0, pattern=[[1, P]], channel_multiplier=-1))
            link(nc.gpsimd.affine_select(out=mask_f[:, 1, :], in_=mask_f[:, 1, :], compare_op=ALU.is_ge, fill=NEG,
                                        base=0, pattern=[[-1, P]], channel_multiplier=1))
            link(nc.gpsimd.memset(k_tok[:, :, R_SHIFT:R_SHIFT + 1], 1.0))
            for r in range(2):
                link(nc.gpsimd.iota(q_tok[:, :, R_BIAS + r:R_BIAS + r + 1], pattern=[[-P, TT], [0, 1]], base=0,
                                   channel_multiplier=-1, allow_small_or_imprecise_dtypes=True))
            link(nc.gpsimd.memset(q_tok[:, :, R_BIAS + 2:R_BIAS + 4], 1.0))
            link(nc.gpsimd.iota(key_no[:], pattern=[[P, TT]], base=0, channel_multiplier=1,
                               allow_small_or_imprecise_dtypes=True))
            link(nc.gpsimd.iota(away[:], pattern=[[P, TT], [-QB, NQB]], base=0, channel_multiplier=1,
                               allow_small_or_imprecise_dtypes=True))
            ytok_rows = y_tok[:].rearrange("p t c -> p (t c)")
            link(nc.gpsimd.iota(ytok_rows[D:D + 2, :], pattern=[[0, NQB], [-1, QB]], base=0, channel_multiplier=0,
                               allow_small_or_imprecise_dtypes=True))
            assert made[0] == GP_CONSTANTS
            gp.wait_ge(s_cv, 2)
            nc.gpsimd.tensor_tensor(u_norm[:, 1, :], u_norm[:, 0, :], half[:], ALU.pow).then_inc(s_pw, 1)

            gp.sem_inc(w_done, 1)
            gp.sem_inc(wp_done, 1)

            def begin(b):
                pass

            def segment(b, main, prep, second, hp):
                for step in steps_of(main, prep, second):
                    if step == ("project", 0):
                        n = b * H + prep
                        gp.wait_ge(w_load, 48 * (n + 1))
                        gp.wait_ge(wg_done, n + 2)
                        gp.wait_ge(pj_full, 1 + NPJ * n)
                        nc.gpsimd.tensor_tensor(w_hi[:], w_in[:], one[:].unsqueeze(2).broadcast_to([P, KC, WCOLS]), ALU.mult).then_inc(w_done, 1)
                        gp.wait_ge(w_done, 1 + 2 * n + 1)
                        nc.gpsimd.tensor_tensor(w_lo[:], w_in[:], w_hi[:].bitcast(F32), ALU.subtract).then_inc(w_done, 1)
                    if step[0] == "square":
                        s = (1 - second) if main is not None else 0
                        n = b * H + prep
                        gp.wait_ge(pj_free, 1 + NPJ * (n + 1))
                        gp.wait_ge(tr_free, 1 + NTR * n)
                        nc.gpsimd.tensor_tensor(k_tok[:, :, 0:D], raw[s][:, :, CK:CK + D],
                                                raw[s][:, :, CK:CK + D], ALU.mult)
                        nc.gpsimd.tensor_tensor(q_tok[:, :, 0:D], raw[s][:, :, CQ:CQ + D],
                                                raw[s][:, :, CQ:CQ + D], ALU.mult).then_inc(sq_done, 1)
                    if step[0] == "sumsq":
                        n = b * H + prep
                        gp.wait_ge(ms_done, n + 2)
                        nc.gpsimd.tensor_tensor(rs[:].rearrange("p a t -> p (a t)"),
                                                mean_sq[:].rearrange("p a t -> p (a t)"), power[:],
                                                ALU.pow).then_inc(rs_done, 1)
                    if step == ("scores", 2) and second == 0:
                        pair = b * (H // 2) + hp
                        gp.wait_ge(wp_load, 16 * (pair + 1))
                        gp.wait_ge(ym_full, 1 + YMB * b + NXT + NQB * NYM * hp)
                        nc.gpsimd.tensor_tensor(wp_hi[:], wp_in[:], one[:, 0:1].broadcast_to([P, C]), ALU.mult).then_inc(wp_done, 1)
                        gp.wait_ge(wp_done, 1 + 2 * pair + 1)
                        nc.gpsimd.tensor_tensor(wp_lo[:], wp_in[:], wp_hi[:].bitcast(F32), ALU.subtract).then_inc(wp_done, 1)

            def end(b):
                gp.wait_ge(lnv_done, b + 1)
                nc.gpsimd.tensor_tensor(ln_rs[:], ln_rs[:], power[:, 0:TT], ALU.pow).then_inc(lnr_done, 1)

            over_heads(gp, segment, begin, end)

        @block.scalar
        def _(act):
            nc.scalar.preload_act_table(ACT.Exp)
            act.wait_ge(s_cv, 4)
            nc.scalar.activation(g[:, 1, :], g[:, 0, :], ACT.Exp).then_inc(s_ce, 1)
            act.sem_inc(pj_free, 1)
            act.sem_inc(qk_hi, 1)
            act.sem_inc(ex_done, BEFORE)

            def begin(b):
                for j in range(NXT):
                    act.wait_ge(ym_full, 1 + YMB * b + j + 1)
                    nc.scalar.activation(xt_hi[:, :, j * 2 * P:(j + 1) * 2 * P],
                                         ps_y[:].rearrange("p (k t) -> p k t", k=KC), ACT.Copy).then_inc(yt_done, 1)

            def segment(b, main, prep, second, hp):
                n = None if main is None else b * H + main
                m = None if prep is None else b * H + prep
                sp_ = (1 - second) if main is not None else 0
                for step in steps_of(main, prep, second):
                    if step[0] == "scores":
                        u_ = step[1]
                        qb, kt = UNITS[u_]
                        off = max(0, kt - TQ * qb) * P
                        act.wait_ge(st_full, NU * n + u_ + 1)
                        act.wait_ge(pv_done, BEFORE + NU * n + u_ + 1 - PR)
                        nc.scalar.activation(exps[:, u_ % PR, off:QB], ps_s[u_ % 2][:, off:QB], ACT.Exp,
                                             bias=bias[second][:, kt, qb:qb + 1]).then_inc(ex_done, 1)
                    if step[0] == "project":
                        j = step[1]
                        act.wait_ge(pj_full, 1 + NPJ * m + j + 1)
                        if j == 0:
                            act.wait_ge(pv_done, BEFORE + NU * (m - 1))
                        nc.scalar.activation(raw[sp_][:, 2 * j:2 * j + 2, 0:ONE],
                                             ps_p[:, 0:2 * WCOLS].rearrange("p (t c) -> p t c", t=2)[:, :, 0:ONE],
                                             ACT.Copy).then_inc(pj_free, 1)
                    if step[0] == "normalise":
                        act.wait_ge(gate, 1 + GATE * m + 3)
                        nc.scalar.activation(g[:, 1, :], g[:, 0, :], ACT.Exp).then_inc(gate_e, 1)
                    if step[0] == "turn":
                        i = step[1]
                        cols = slice((i // 2) * QB, (i // 2 + 1) * QB)
                        dst = (k_ext, q_max)[i % 2][sp_]
                        act.wait_ge(tr_full, 1 + NTR * m + i + 1)
                        nc.scalar.activation(dst[:, cols], ps_t[:], ACT.Copy).then_inc(qk_hi, 1)
                    if step[0] == "out" and step[2] == 0:
                        qb = step[1]
                        act.wait_ge(ym_full, 1 + YMB * b + NXT + NQB * NYM * hp + NYM * qb + 1)
                        nc.scalar.activation(yt_hi[:], ps_y[:], ACT.Copy).then_inc(yt_done, 1)

            def end(b):
                pass

            over_heads(act, segment, begin, end)

        YTB = NXT + (H // 2) * NQB

        @block.vector
        def _(dve):
            def softplus(link, x_ap, out_ap):
                e, s, z, p, r = (g[:, i, :] for i in (1, 2, 3, 4, 5))
                link(nc.vector.tensor_scalar(s, e, 2.0, None, ALU.add))
                link(nc.vector.reciprocal(r, s))
                link(nc.vector.tensor_tensor(s, e, r, ALU.mult))
                link(nc.vector.tensor_tensor(z, s, s, ALU.mult))
                link(nc.vector.tensor_scalar(p, z, 1.0 / 15, None, ALU.mult))
                for k in (13, 11, 9, 7, 5, 3):
                    link(nc.vector.scalar_tensor_tensor(p, p, 1.0 / k, z, ALU.add, ALU.mult))
                link(nc.vector.scalar_tensor_tensor(p, p, 1.0, s, ALU.add, ALU.mult))
                link(nc.vector.tensor_scalar(r, x_ap, 0.0, None, ALU.max))
                link(nc.vector.scalar_tensor_tensor(out_ap, p, 2.0, r, ALU.mult, ALU.add))

            count = [0]

            def link(ins):
                count[0] += 1
                ins.then_inc(s_cv, 1)
                dve.wait_ge(s_cv, count[0])

            dve.wait_ge(s_par, 64)
            dve.wait_ge(s_cg, GP_CONSTANTS)
            link(nc.vector.tensor_tensor(exps[:, 0:2, :].rearrange("p a (h d) -> p (a h) d", d=D), u_gate[:], u_gate[:], ALU.mult))
            link(nc.vector.tensor_reduce(u_norm[:, 0, :], exps[:, 0:2, :].rearrange("p a (h d) -> p (a h) d", d=D), AX.X, ALU.add))
            link(nc.vector.tensor_scalar(g[:, 6, :], omega_eff[:], 0.0, None, ALU.add))
            link(nc.vector.scalar_tensor_tensor(g[:, 0, :], g[:, 6, :], -1.0, g[:, 6, :], ALU.mult, ALU.min))
            dve.wait_ge(s_ce, 1)
            softplus(link, g[:, 6, :], g[:, 7, :])
            link(nc.vector.tensor_tensor(omega_eff[:], g[:, 7, :], slopes[:], ALU.mult))
            dve.wait_ge(s_pw, 1)
            link(nc.vector.tensor_scalar(u_norm[:, 0, :], u_norm[:, 1, :], EPS_U, None, ALU.max))
            link(nc.vector.reciprocal(u_norm[:, 1, :], u_norm[:, 0, :]))
            link(nc.vector.tensor_tensor(u_gate[:], u_gate[:], u_norm[:, 1, :].unsqueeze(2).broadcast_to([P, H, D]), ALU.mult))
            link(nc.vector.tensor_scalar(rms_in[:, 1, :], rms_in[:, 1, :], D ** -0.5, None, ALU.mult))
            link(nc.vector.tensor_tensor(u_gate[:], u_gate[:], rms_in[:, 1:2, :].broadcast_to([P, H, D]), ALU.mult))
            link(nc.vector.tensor_tensor(qk_w[:], rms_in[:, 0, :], rms_in[:, 1, :], ALU.mult))
            nc.vector.tensor_copy(ident_r[:], ident[:])
            nc.vector.tensor_copy(mask_kq[:], mask_f[:, 0, :])
            nc.vector.tensor_copy(mask_qk[:], mask_f[:, 1, :])
            rows = y_tok[:].rearrange("p t c -> p (t c)")
            for i in range(2):
                link(nc.vector.tensor_copy(q_ext[i][D:P, :], q_tok[D:P, :, R_BIAS + 4:R_BIAS + 5].broadcast_to([D, TT, P])))
                link(nc.vector.tensor_copy(q_ext[i][D:D + 2, :], rows[D:D + 2, :]))
            nc.vector.memset(mean_sq[:], 1.0).then_inc(s_const, 1)
            dve.sem_inc(wg_done, 1)
            dve.sem_inc(ms_done, 1)
            dve.sem_inc(gate, 1)
            dve.sem_inc(tr_free, 1)
            dve.sem_inc(mx_free, 2)
            dve.sem_inc(nm_done, 1)
            dve.sem_inc(y_done, 1)
            dve.sem_inc(ym_free, 1)
            dve.sem_inc(nrm, 1)
            dve.wait_ge(s_const, 1)

            def begin(b):
                for j in range(NXT):
                    dve.wait_ge(yt_done, YTB * b + j + 1)
                    cols = slice(j * 2 * P, (j + 1) * 2 * P)
                    nc.vector.tensor_tensor(xt_lo[:, :, cols], ps_y[:].rearrange("p (k t) -> p k t", k=KC),
                                            xt_hi[:, :, cols].bitcast(F32), ALU.subtract).then_inc(ym_free, 1)

            def segment(b, main, prep, second, hp):
                n = None if main is None else b * H + main
                m = None if prep is None else b * H + prep
                s = (1 - second) if main is not None else 0
                for step in steps_of(main, prep, second):
                    if step == ("project", 0):
                        dve.wait_ge(w_load, 48 * (m + 1))
                        dve.wait_ge(wg_done, m + 1)
                        nc.vector.tensor_tensor(wg_tmp[:], w_in[:, :, CK:CK + D],
                                                u_gate[:, bass.ds(prep, 1), :].broadcast_to([P, KC, D]), ALU.mult).then_inc(wg_t, 1)
                        dve.wait_ge(wg_t, m + 1)
                        nc.vector.tensor_reduce(w_in[:, :, CG:CG + 1], wg_tmp[:], AX.X, ALU.add).then_inc(wg_done, 1)
                    if step[0] == "sumsq":
                        dve.wait_ge(sq_done, m + 1)
                        nc.vector.tensor_reduce(sumsq[:, 0, :], k_tok[:, :, 0:D], AX.X, ALU.add)
                        nc.vector.tensor_reduce(sumsq[:, 1, :], q_tok[:, :, 0:D], AX.X, ALU.add).then_inc(ss_part, 1)
                        dve.wait_ge(ss_part, m + 1)
                        nc.vector.tensor_scalar(mean_sq[:], sumsq[:], 1.0 / D, EPS_RMS, ALU.mult, ALU.add).then_inc(ms_done, 1)
                    if step[0] == "normalise":
                        dve.wait_ge(rs_done, m + 1)
                        gcount = [0]

                        def glink(ins):
                            gcount[0] += 1
                            ins.then_inc(gate, 1)
                            dve.wait_ge(gate, 1 + GATE * m + gcount[0])

                        glink(nc.vector.tensor_tensor(q_tok[:, :, 0:D], raw[s][:, :, CQ:CQ + D],
                                                      rs[:, 1, :].unsqueeze(2).broadcast_to([P, TT, D]), ALU.mult))
                        glink(nc.vector.tensor_tensor(g[:, 6, :], raw[s][:, :, CG], rs[:, 0, :], ALU.mult))
                        glink(nc.vector.scalar_tensor_tensor(g[:, 0, :], g[:, 6, :], -1.0, g[:, 6, :], ALU.mult, ALU.min))
                        glink(nc.vector.tensor_tensor(k_tok[:, :, 0:D], raw[s][:, :, CK:CK + D],
                                                      rs[:, 0, :].unsqueeze(2).broadcast_to([P, TT, D]), ALU.mult))
                        glink(nc.vector.tensor_tensor(q_tok[:, :, 0:D], q_tok[:, :, 0:D],
                                                      qk_w[:].unsqueeze(1).broadcast_to([P, TT, D]), ALU.mult))
                        dve.wait_ge(gate_e, m + 1)
                        softplus(glink, g[:, 6, :], g[:, 7, :])
                        c, jc = k_tok[:, :, R_BIAS], k_tok[:, :, R_BIAS + 2]
                        glink(nc.vector.tensor_scalar(c, g[:, 7, :], omega_eff[:, bass.ds(prep, 1)], None, ALU.mult))
                        glink(nc.vector.tensor_tensor(jc, c, key_no[:], ALU.mult))
                        nc.vector.tensor_copy(c_hi[:], c)
                        glink(nc.vector.tensor_copy(jc_hi[:], jc))
                        dve.wait_ge(ex_done, BEFORE + NU * (m - 1))
                        nc.vector.tensor_tensor(bias[s][:], away[:], c.unsqueeze(2).broadcast_to([P, TT, NQB]), ALU.mult)
                        nc.vector.tensor_tensor(k_tok[:, :, R_BIAS + 1], c, c_hi[:].bitcast(F32), ALU.subtract)
                        glink(nc.vector.tensor_tensor(k_tok[:, :, R_BIAS + 3], jc, jc_hi[:].bitcast(F32), ALU.subtract))
                        while gcount[0] < GATE:
                            glink(nc.vector.tensor_copy(g[:, 9, 0:1], g[:, 7, 0:1]))
                        assert gcount[0] == GATE
                    if step[0] == "turn":
                        i = step[1]
                        cols = slice((i // 2) * QB, (i // 2 + 1) * QB)
                        dve.wait_ge(qk_hi, 1 + 2 * NQB * m + i + 1)
                        dst, hi = ((k_split[s][D:P, cols], k_ext[s]), (q_ext[s][0:D, cols], q_max[s]))[i % 2]
                        nc.vector.tensor_tensor(dst, ps_t[0:D, :], hi[0:D, cols].bitcast(F32), ALU.subtract).then_inc(tr_free, 1)
                    if step[0] == "max":
                        v = step[1]
                        qt, kc = MAXES[v]
                        width = min(QB, (qt + 1) * P - kc * QB)
                        dve.wait_ge(mx_full, NM * m + v + 1)
                        if v == 0:
                            dve.wait_ge(nm_done, 1 + NQB * m)
                        nc.vector.tensor_reduce(maxes[:, qt, kc:kc + 1], ps_m[v % 2][:, 0:width], AX.X, ALU.max).then_inc(mx_free, 1)
                    if step[0] == "negmax":
                        qb = step[1]
                        dve.wait_ge(mx_free, 2 + NM * m + group_end(qb))
                        nc.vector.tensor_reduce(neg_max[:, qb * TQ:(qb + 1) * TQ], maxes[:, qb * TQ:(qb + 1) * TQ, 0:qb + 1],
                                                AX.X, ALU.max, negate=True).then_inc(nm_done, 1)
                    if step[0] == "shift":
                        qb = step[1]
                        dve.wait_ge(tr_full, 1 + NTR * m + 2 * NQB + qb + 1)
                        nc.vector.tensor_copy(q_ext[s][R_SHIFT:R_SHIFT + 1, qb * QB:(qb + 1) * QB],
                                              ps_t[R_SHIFT:R_SHIFT + 1, :]).then_inc(tr_free, 1)
                    if step[0] == "divide":
                        qb = step[1]
                        pv = ps_v[:, 0:TQ * (D + 1)].rearrange("p (t c) -> p t c", t=TQ)
                        dve.wait_ge(pv_done, BEFORE + NU * n + len([1 for q, _ in UNITS if q <= qb]))
                        dve.wait_ge(y_done, 1 + NQB * n + qb)
                        nc.vector.reciprocal(recip[:], pv[:, :, D]).then_inc(rc_done, 1)
                        dve.wait_ge(rc_done, NQB * n + qb + 1)
                        nc.vector.tensor_tensor(y_tok[:, qb * TQ:(qb + 1) * TQ, second * D:(second + 1) * D],
                                                pv[:, :, 0:D], recip[:].unsqueeze(2).broadcast_to([P, TQ, D]), ALU.mult).then_inc(y_done, 1)
                    if step[0] == "out":
                        qb, i = step[1], step[2]
                        if i == 0:
                            dve.wait_ge(yt_done, YTB * b + NXT + NQB * hp + qb + 1)
                            nc.vector.tensor_tensor(yt_lo[:], ps_y[:], yt_hi[:].bitcast(F32), ALU.subtract).then_inc(ym_free, 1)
                        else:
                            t0 = qb * TQ + 2 * (i - 1)
                            dve.wait_ge(ym_full, 1 + YMB * b + NXT + NQB * NYM * hp + NYM * qb + i + 1)
                            nc.vector.tensor_tensor(acc[:, t0:t0 + 2, :], acc[:, t0:t0 + 2, :],
                                                    ps_y[:].rearrange("p (t c) -> p t c", t=2), ALU.add).then_inc(ym_free, 1)

            def end(b):
                dve.wait_ge(ym_free, 1 + YMB * (b + 1))
                for t in range(TT):
                    last = nc.vector.bn_stats(stats[:, t, :], acc[:, t, :])
                last.then_inc(bn_done, 1)
                dve.wait_ge(bn_done, 2 * b + 1)
                nc.vector.memset(recip[:], 1.0)
                for t in range(TT):
                    last = nc.vector.bn_aggr(mean_var[:, t, :], stats[:, t, :])
                last.then_inc(bn_done, 1)
                dve.wait_ge(bn_done, 2 * b + 2)
                nc.vector.tensor_scalar(ln_rs[:], mean_var[:, :, 1], EPS_LN, None, ALU.add).then_inc(lnv_done, 1)
                dve.wait_ge(lnr_done, b + 1)
                for t in range(TT):
                    last = nc.vector.tensor_scalar(acc[:, t, :], acc[:, t, :], mean_var[:, t, 0:1], ln_rs[:, t:t + 1],
                                                   ALU.subtract, ALU.mult)
                last.then_inc(ln_done, 1)
                dve.wait_ge(ln_done, b + 1)

            over_heads(dve, segment, begin, end)

        @block.tensor
        def _(pe):
            pe.wait_ge(s_const, 1)
            pe.sem_inc(pj_full, 1)
            pe.sem_inc(tr_full, 1)
            pe.sem_inc(ym_full, 1)
            pe.sem_inc(pv_done, BEFORE)

            def begin(b):
                pe.wait_ge(x_in, 16 * (b + 1))
                for j in range(NXT):
                    pe.wait_ge(ym_free, 1 + YMB * b + j)
                    for k in range(KC):
                        for t in range(2):
                            last = nc.tensor.transpose(ps_y[:, (2 * k + t) * P:(2 * k + t + 1) * P],
                                                       acc[:, 2 * j + t, k * P:(k + 1) * P], ident[:])
                    last.then_inc(ym_full, 1)

            def split_product(out, pairs):
                terms = [(a, c) for (ah, al), (ch, cl) in pairs for a, c in ((ah, ch), (ah, cl), (al, ch))]
                for i, (a, c) in enumerate(terms):
                    last = nc.tensor.matmul(out, a, c, start=i == 0, stop=i == len(terms) - 1)
                return last

            def segment(b, main, prep, second, hp):
                n = None if main is None else b * H + main
                m = None if prep is None else b * H + prep
                s = (1 - second) if main is not None else 0
                for step in steps_of(main, prep, second):
                    if step[0] == "scores":
                        u_ = step[1]
                        qb, kt = UNITS[u_]
                        diag = kt >= TQ * qb
                        off = max(0, kt - TQ * qb) * P
                        if kt == 0:
                            pe.wait_ge(tr_free, 1 + NTR * n + 2 * NQB + qb + 1)
                            pe.wait_ge(dup[qb], 48 * (n + 1))
                        pe.wait_ge(ex_done, BEFORE + NU * n + u_ + 1 - 2)
                        out = ps_s[u_ % 2][:, off:QB]
                        q = slice(qb * QB + off, (qb + 1) * QB)
                        k = slice(kt * P, (kt + 1) * P)
                        nc.tensor.matmul(out, k_split[second][:, k], q_twice[second][:, q], start=True, stop=False)
                        last = nc.tensor.matmul(out, k_ext[second][:, k], q_ext[second][:, q], start=False, stop=not diag)
                        if diag:
                            last = nc.tensor.matmul(ps_s[u_ % 2][:, off:off + P], ident_r[:], mask_kq[:], start=False, stop=True)
                        last.then_inc(st_full, 1)
                    if step[0] == "values":
                        u_ = step[1]
                        qb, kt = UNITS[u_]
                        pe.wait_ge(ex_done, BEFORE + NU * n + u_ + 1)
                        if kt == 0:
                            pe.wait_ge(y_done, 1 + NQB * n + qb)
                        for t in range(max(0, kt - TQ * qb), TQ):
                            last = nc.tensor.matmul(ps_v[:, t * (D + 1):(t + 1) * (D + 1)],
                                                    exps[:, u_ % PR, t * P:(t + 1) * P],
                                                    raw[second][:, kt, CV:CV + D + 1],
                                                    start=(kt == 0 and t == 0), stop=(kt == TQ * qb + t),
                                                    skip_group_check=True)
                        last.then_inc(pv_done, 1)
                    if step[0] == "project":
                        j = step[1]
                        if j == 0:
                            pe.wait_ge(w_done, 1 + 2 * (m + 1))
                            pe.wait_ge(ym_free, 1 + YMB * b + NXT)
                        pe.wait_ge(pj_free, 1 + NPJ * m + j)
                        for t in range(2):
                            tok = slice((2 * j + t) * P, (2 * j + t + 1) * P)
                            last = split_product(ps_p[:, t * WCOLS:(t + 1) * WCOLS],
                                                 [((xt_hi[:, k, tok], xt_lo[:, k, tok]), (w_hi[:, k, :], w_lo[:, k, :]))
                                                  for k in range(KC)])
                        last.then_inc(pj_full, 1)
                    if step[0] == "turn":
                        i = step[1]
                        if i == 0:
                            pe.wait_ge(gate, 1 + GATE * (m + 1))
                        pe.wait_ge(tr_free, 1 + NTR * m + i)
                        src = (k_tok, q_tok)[i % 2]
                        for t in range(TQ):
                            last = nc.tensor.transpose(ps_t[:, t * P:(t + 1) * P], src[:, (i // 2) * TQ + t, :], ident[:])
                        last.then_inc(tr_full, 1)
                    if step[0] == "max":
                        v = step[1]
                        qt, kc = MAXES[v]
                        if kc == 0 and qt % TQ == 0:
                            pe.wait_ge(qk_hi, 1 + 2 * NQB * m + 2 * (qt // TQ) + 2)
                        pe.wait_ge(mx_free, 2 + NM * m + v + 1 - 2)
                        width = min(QB, (qt + 1) * P - kc * QB)
                        diag = kc == qt // TQ
                        last = nc.tensor.matmul(ps_m[v % 2][:, 0:width], q_max[s][:, qt * P:(qt + 1) * P],
                                                k_ext[s][:, kc * QB:kc * QB + width], start=True, stop=not diag)
                        if diag:
                            last = nc.tensor.matmul(ps_m[v % 2][:, width - P:width], ident_r[:], mask_qk[:], start=False, stop=True)
                        last.then_inc(mx_full, 1)
                    if step[0] == "shift":
                        qb = step[1]
                        pe.wait_ge(nm_done, 1 + NQB * m + qb + 1)
                        pe.wait_ge(tr_free, 1 + NTR * m + 2 * NQB + qb)
                        for t in range(TQ):
                            col = neg_max[:, qb * TQ + t:qb * TQ + t + 1]
                            last = nc.tensor.matmul(ps_t[:, t * P:(t + 1) * P], col.broadcast_to([P, P]), ident_r[:],
                                                    start=True, stop=True)
                        last.then_inc(tr_full, 1)
                    if step[0] == "out":
                        qb, i = step[1], step[2]
                        pe.wait_ge(ym_free, 1 + YMB * b + NXT + NQB * NYM * hp + NYM * qb + i)
                        if i == 0:
                            pe.wait_ge(y_done, 1 + NQB * n + qb + 1)
                            for t in range(TQ):
                                last = nc.tensor.transpose(ps_y[:, t * P:(t + 1) * P], y_tok[:, qb * TQ + t, :], ident[:])
                        else:
                            if qb == 0:
                                pe.wait_ge(wp_done, 1 + 2 * (b * (H // 2) + hp + 1))
                            for t in range(2):
                                tok = slice((2 * (i - 1) + t) * P, (2 * (i - 1) + t + 1) * P)
                                last = split_product(ps_y[:, t * C:(t + 1) * C], [((yt_hi[:, tok], yt_lo[:, tok]), (wp_hi[:], wp_lo[:]))])
                        last.then_inc(ym_full, 1)

            over_heads(pe, segment, begin, lambda b: None)



NTOK = 512
NBLK = B * T // NTOK
OC = HID // P
NT = NTOK // P
STAGES = 4
AR = 4


def split_sum(nc, out, pairs):
    terms = [(a, c) for (ah, al), (ch, cl) in pairs for a, c in ((ah, ch), (ah, cl), (al, ch))]
    for i, (a, c) in enumerate(terms):
        last = nc.tensor.matmul(out, a, c, start=i == 0, stop=i == len(terms) - 1)
    return last


def stage_target(item, half, table):
    hi, lo, row, narrow = table[item]
    if narrow:
        cut = slice((row + 2 * half) * P, (row + 2 * half + 2) * P)
        return [w[:, :, cut].rearrange("p k (o c) -> p o k c", o=2) for w in (hi, lo)]
    return [w[:, 4 * half:4 * half + 4, row * P:(row + 1) * P] for w in (hi, lo)]


def ffn_up(nc, x1_dram, w1_w, w1_s, w2_w, w2_s, h1_w, h1_s, a_dram):
    ctx = ExitStack()
    with ctx:
        def sb(name, shape, dt=F32):
            return ctx.enter_context(nc.sbuf_tensor(name, shape, dt))

        def pb(name):
            return ctx.enter_context(nc.psum_tensor(name, [P, 512], F32))

        def sem(name):
            return ctx.enter_context(nc.semaphore(name))

        ident = sb("up_ident", [P, P])
        stage = [sb(f"up_stage{i}", [P, 8 * P]) for i in range(STAGES)]
        w1_hi, w1_lo = sb("w1_hi", [P, KC, HID], F32R), sb("w1_lo", [P, KC, HID], F32R)
        w2_hi, w2_lo = sb("w2_hi", [P, KC, HID], F32R), sb("w2_lo", [P, KC, HID], F32R)
        h1_hi, h1_lo = sb("h1_hi", [P, OC, HID], F32R), sb("h1_lo", [P, OC, HID], F32R)
        scale = sb("up_scale", [P, 3, OC])
        x_tok = sb("x_tok", [P, NT, C])
        x_hi, x_lo = sb("x_hi", [P, KC, NTOK], F32R), sb("x_lo", [P, KC, NTOK], F32R)
        silu = sb("silu", [P, 2, NTOK])
        prod = sb("prod", [P, 2, NTOK])
        p_hi, p_lo = sb("p_hi", [P, OC, NTOK], F32R), sb("p_lo", [P, OC, NTOK], F32R)
        gelu = sb("gelu", [P, AR, NTOK])

        ps_t = [pb(f"up_t{i}") for i in range(2)]
        ps_1 = [pb(f"up_1{i}") for i in range(2)]
        ps_2 = [pb(f"up_2{i}") for i in range(2)]
        ps_h = [pb(f"up_h{i}") for i in range(2)]

        par = sem("up_par")
        made = sem("up_made")
        staged = [sem(f"up_staged{i}") for i in range(STAGES)]
        wt_full = sem("up_wt_full")
        wt_hi = sem("up_wt_hi")
        wt_free = sem("up_wt_free")
        x_load = sem("up_x_load")
        xt_full = sem("up_xt_full")
        xt_hi = sem("up_xt_hi")
        xt_free = sem("up_xt_free")
        l1_full = sem("up_l1_full")
        silu_done = sem("up_silu_done")
        l1_free = sem("up_l1_free")
        hi_done = sem("up_hi_done")
        lo_done = sem("up_lo_done")
        l2_full = sem("up_l2_full")
        gelu_done = sem("up_gelu_done")
        stored = [sem(f"up_stored{i}") for i in range(AR)]

        table = [(w1_hi, w1_lo, 4 * i, True) for i in range(2)] + [(w2_hi, w2_lo, 4 * i, True) for i in range(2)] \
            + [(h1_hi, h1_lo, i, False) for i in range(OC)]
        rows = [(w, slice(4 * i * P, 4 * (i + 1) * P)) for w in (w1_w, w2_w) for i in range(2)] \
            + [(h1_w, slice(i * P, (i + 1) * P)) for i in range(OC)]
        NW = 2 * len(table)

        def over_blocks(eng, turn_x, body):
            turn_x(0)
            with eng.Fori(0, NBLK - 1) as i:
                body(i, True)
            body(NBLK - 1, False)

        block = ctx.enter_context(nc.Block())

        def load_x(sp, i):
            sp.dma_start(x_tok[:], x1_dram[bass.ds(i * NTOK, NTOK), :].rearrange("(t p) c -> p t c", p=P)).then_inc(x_load, 16)

        def sp_body(i, more):
            sp = nc.sync
            if more:
                sp.wait_ge(xt_full, 2 * (i + 1))
                load_x(sp, i + 1)
            for o in range(OC):
                sp.wait_ge(gelu_done, 2 + OC * i + o + 1)
                sp.dma_start(a_dram[o * P:(o + 1) * P, bass.ds(i * NTOK, NTOK)], gelu[:, o % AR, :]).then_inc(stored[o % AR], 16)

        @block.sync
        def _(sp):
            for i, s in enumerate((w1_s, w2_s, h1_s)):
                sp.dma_start(scale[:, i, :], s.rearrange("(o p) -> p o", p=P), allow_slow_non_contiguous=True).then_inc(par, 16)
            for i, (w, cut) in enumerate(rows):
                if i >= STAGES:
                    sp.wait_ge(wt_full, 2 * (i - STAGES + 1))
                sp.dma_start(stage[i % STAGES][:].rearrange("p (r c) -> p r c", c=w.shape[1]),
                             w[cut, :].rearrange("(r p) c -> p r c", p=P)).then_inc(staged[i % STAGES], 16)
                if i == 3:
                    load_x(sp, 0)
            over_blocks(sp, lambda i: None, sp_body)
            for s in stored:
                sp.wait_ge(s, 1 + 16 * (OC // AR) * NBLK)

        @block.gpsimd
        def _(gp):
            nc.gpsimd.memset(ident[:], 0.0).then_inc(made, 1)
            gp.wait_ge(made, 1)
            nc.gpsimd.affine_select(out=ident[:], in_=ident[:], compare_op=ALU.not_equal, fill=1.0, base=0,
                                    pattern=[[-1, P]], channel_multiplier=1).then_inc(made, 1)

        @block.scalar
        def _(act):
            act.sem_inc(gelu_done, 2)
            for s in stored:
                act.sem_inc(s, 1)
            for r in range(NW):
                act.wait_ge(wt_full, r + 1)
                out = stage_target(r // 2, r % 2, table)[0]
                src = ps_t[r % 2][:].rearrange("p (o k c) -> p o k c", o=2, k=2) if table[r // 2][3] \
                    else ps_t[r % 2][:].rearrange("p (k c) -> p k c", k=4)
                nc.scalar.activation(out, src, ACT.Copy).then_inc(wt_hi, 1)

            def turn_x(i):
                for e in range(2):
                    act.wait_ge(xt_full, 2 * i + e + 1)
                    nc.scalar.activation(x_hi[:, :, 2 * e * P:2 * (e + 1) * P],
                                         ps_t[e][:].rearrange("p (k t) -> p k t", k=KC), ACT.Copy).then_inc(xt_hi, 1)

            def body(i, more):
                for o in range(OC):
                    act.wait_ge(l1_full, OC * i + o + 1)
                    if o == 0:
                        act.wait_ge(par, 48)
                    nc.scalar.activation(silu[:, o % 2, :], ps_1[o % 2][:], ACT.Silu, scale=scale[:, 0, o:o + 1]).then_inc(silu_done, 1)
                    act.wait_ge(l1_free, 2 + OC * i + o + 1)
                    nc.scalar.activation(p_hi[:, o, :], prod[:, o % 2, :], ACT.Copy).then_inc(hi_done, 1)
                for o in range(OC):
                    if o == 3 and more:
                        turn_x(i + 1)
                    act.wait_ge(l2_full, OC * i + o + 1)
                    act.wait_ge(stored[o % AR], 1 + 16 * ((OC // AR) * i + o // AR))
                    nc.scalar.activation(gelu[:, o % AR, :], ps_h[o % 2][:], ACT.Gelu, scale=scale[:, 2, o:o + 1]).then_inc(gelu_done, 1)

            over_blocks(act, turn_x, body)

        @block.vector
        def _(dve):
            dve.sem_inc(xt_free, 2)
            dve.sem_inc(l1_free, 2)
            dve.sem_inc(lo_done, 2)
            for r in range(NW):
                dve.wait_ge(wt_hi, r + 1)
                hi, lo = stage_target(r // 2, r % 2, table)
                src = ps_t[r % 2][:].rearrange("p (o k c) -> p o k c", o=2, k=2) if table[r // 2][3] \
                    else ps_t[r % 2][:].rearrange("p (k c) -> p k c", k=4)
                nc.vector.tensor_tensor(lo, src, hi.bitcast(F32), ALU.subtract).then_inc(wt_free, 1)
            dve.wait_ge(par, 48)

            def turn_x(i):
                for e in range(2):
                    dve.wait_ge(xt_hi, 2 * i + e + 1)
                    cut = slice(2 * e * P, 2 * (e + 1) * P)
                    nc.vector.tensor_tensor(x_lo[:, :, cut], ps_t[e][:].rearrange("p (k t) -> p k t", k=KC),
                                            x_hi[:, :, cut].bitcast(F32), ALU.subtract).then_inc(xt_free, 1)

            def body(i, more):
                for o in range(OC):
                    dve.wait_ge(silu_done, OC * i + o + 1)
                    dve.wait_ge(lo_done, 2 + OC * i + o - 1)
                    nc.vector.scalar_tensor_tensor(prod[:, o % 2, :], ps_2[o % 2][:], scale[:, 1, o:o + 1], silu[:, o % 2, :],
                                                   ALU.mult, ALU.mult).then_inc(l1_free, 1)
                    dve.wait_ge(hi_done, OC * i + o + 1)
                    nc.vector.tensor_tensor(p_lo[:, o, :], prod[:, o % 2, :], p_hi[:, o, :].bitcast(F32), ALU.subtract).then_inc(lo_done, 1)
                if more:
                    turn_x(i + 1)

            over_blocks(dve, turn_x, body)

        @block.tensor
        def _(pe):
            pe.wait_ge(made, 2)
            for r in range(NW):
                pe.wait_ge(staged[(r // 2) % STAGES], 16 * (r // 2 // STAGES + 1))
                if r >= 2:
                    pe.wait_ge(wt_free, r - 1)
                for q in range(4):
                    last = nc.tensor.transpose(ps_t[r % 2][:, q * P:(q + 1) * P],
                                               stage[(r // 2) % STAGES][:, (4 * (r % 2) + q) * P:(4 * (r % 2) + q + 1) * P], ident[:])
                last.then_inc(wt_full, 1)
            pe.wait_ge(wt_free, NW)

            def turn_x(i):
                pe.wait_ge(x_load, 16 * (i + 1))
                for e in range(2):
                    pe.wait_ge(xt_free, 2 * i + e + 1)
                    for k in range(KC):
                        for t in range(2):
                            last = nc.tensor.transpose(ps_t[e][:, (2 * k + t) * P:(2 * k + t + 1) * P],
                                                       x_tok[:, 2 * e + t, k * P:(k + 1) * P], ident[:])
                    last.then_inc(xt_full, 1)

            def body(i, more):
                for o in range(OC):
                    col = slice(o * P, (o + 1) * P)
                    if o == 0:
                        pe.wait_ge(xt_free, 2 + 2 * (i + 1))
                    pe.wait_ge(l1_free, 2 + OC * i + o - 1)
                    split_sum(nc, ps_1[o % 2][:], [((w1_hi[:, k, col], w1_lo[:, k, col]), (x_hi[:, k, :], x_lo[:, k, :])) for k in range(KC)])
                    split_sum(nc, ps_2[o % 2][:], [((w2_hi[:, k, col], w2_lo[:, k, col]), (x_hi[:, k, :], x_lo[:, k, :]))
                                                   for k in range(KC)]).then_inc(l1_full, 1)
                for o in range(OC):
                    col = slice(o * P, (o + 1) * P)
                    if o == 3 and more:
                        turn_x(i + 1)
                    pe.wait_ge(gelu_done, 2 + OC * i + o - 1)
                    for k in range(OC):
                        if o == 0:
                            pe.wait_ge(lo_done, 2 + OC * i + k + 1)
                        for j, (w, p) in enumerate(((h1_hi, p_hi), (h1_lo, p_hi), (h1_hi, p_lo))):
                            last = nc.tensor.matmul(ps_h[o % 2][:], w[:, k, col], p[:, k, :], start=k == 0 and j == 0,
                                                    stop=k == OC - 1 and j == 2)
                    last.then_inc(l2_full, 1)

            over_blocks(pe, turn_x, body)


def ffn_down(nc, a_dram, x1_dram, h2_w, h2_s, w3_w, w3_s, out):
    ctx = ExitStack()
    with ctx:
        def sb(name, shape, dt=F32):
            return ctx.enter_context(nc.sbuf_tensor(name, shape, dt))

        def pb(name):
            return ctx.enter_context(nc.psum_tensor(name, [P, 512], F32))

        def sem(name):
            return ctx.enter_context(nc.semaphore(name))

        ident = sb("dn_ident", [P, P])
        stage = [sb(f"dn_stage{i}", [P, 8 * P]) for i in range(2)]
        h2_hi, h2_lo = sb("h2_hi", [P, OC, HID], F32R), sb("h2_lo", [P, OC, HID], F32R)
        w3_hi, w3_lo = sb("w3_hi", [P, OC, C], F32R), sb("w3_lo", [P, OC, C], F32R)
        scale = sb("dn_scale", [P, OC])
        scale_out = sb("dn_scale_out", [P, C])
        a_in = sb("a_in", [P, OC, NTOK])
        a_hi, a_lo = sb("a_hi", [P, OC, NTOK], F32R), sb("a_lo", [P, OC, NTOK], F32R)
        gelu = sb("dn_gelu", [P, 2, NTOK])
        b_hi, b_lo = sb("b_hi", [P, OC, NTOK], F32R), sb("b_lo", [P, OC, NTOK], F32R)
        x_tok = sb("dn_x", [P, NT, C])
        y = sb("dn_y", [P, NT, C])
        stats = sb("dn_stats", [P, NT, 6])
        mean_var = sb("dn_mean_var", [P, NT, 2])
        rs = sb("dn_rs", [P, 2, NT])
        power = sb("dn_power", [P, NT])

        ps_t = [pb(f"dn_t{i}") for i in range(2)]
        ps_h = [pb(f"dn_h{i}") for i in range(2)]
        ps_o = [pb(f"dn_o{i}") for i in range(2)]

        par = sem("dn_par")
        made = sem("dn_made")
        staged = [sem(f"dn_staged{i}") for i in range(2)]
        wt_full = sem("dn_wt_full")
        wt_hi = sem("dn_wt_hi")
        wt_free = sem("dn_wt_free")
        a_load = sem("dn_a_load")
        x_load = sem("dn_x_load")
        ahi_done = sem("dn_ahi_done")
        alo_done = sem("dn_alo_done")
        l3_full = sem("dn_l3_full")
        gelu_done = sem("dn_gelu_done")
        bhi_done = sem("dn_bhi_done")
        blo_done = sem("dn_blo_done")
        l4_full = sem("dn_l4_full")
        l4_free = sem("dn_l4_free")
        sum_done = sem("dn_sum_done")
        bn_done = sem("dn_bn_done")
        var_done = sem("dn_var_done")
        rs_done = sem("dn_rs_done")
        ln_done = sem("dn_ln_done")
        out_done = sem("dn_out_done")

        table = [(h2_hi, h2_lo, i, False) for i in range(OC)] + [(w3_hi, w3_lo, i, False) for i in range(KC)]
        rows = [(h2_w, slice(i * P, (i + 1) * P)) for i in range(OC)] + [(w3_w, slice(i * P, (i + 1) * P)) for i in range(KC)]
        NW = 2 * len(table)

        def over_blocks(eng, split_a, body):
            split_a(0)
            with eng.Fori(0, NBLK - 1) as i:
                body(i, True)
            body(NBLK - 1, False)

        block = ctx.enter_context(nc.Block())

        def load_a(sp, i):
            sp.dma_start(a_in[:], a_dram[:, bass.ds(i * NTOK, NTOK)].rearrange("(k p) n -> p k n", p=P)).then_inc(a_load, 16)

        def sp_body(i, more):
            sp = nc.sync
            sp.wait_ge(sum_done, 1 + NT * i)
            sp.dma_start(x_tok[:], x1_dram[bass.ds(i * NTOK, NTOK), :].rearrange("(t p) c -> p t c", p=P)).then_inc(x_load, 16)
            if more:
                sp.wait_ge(alo_done, 1 + OC * (i + 1))
                load_a(sp, i + 1)
            sp.wait_ge(ln_done, i + 1)
            sp.dma_start(out[bass.ds(i * NTOK, NTOK), :].rearrange("(t p) c -> p t c", p=P), y[:]).then_inc(out_done, 16)

        @block.sync
        def _(sp):
            sp.dma_start(scale[:], h2_s.rearrange("(o p) -> p o", p=P), allow_slow_non_contiguous=True).then_inc(par, 16)
            sp.dma_start(scale_out[:], w3_s.partition_broadcast(P)).then_inc(par, 16)
            for i, (w, cut) in enumerate(rows):
                if i >= 2:
                    sp.wait_ge(wt_full, 2 * (i - 1))
                sp.dma_start(stage[i % 2][:], w[cut, :]).then_inc(staged[i % 2], 16)
                if i == 1:
                    load_a(sp, 0)
            over_blocks(sp, lambda i: None, sp_body)
            sp.wait_ge(out_done, 1 + 16 * NBLK)

        @block.gpsimd
        def _(gp):
            nc.gpsimd.memset(power[:], -0.5)
            nc.gpsimd.memset(ident[:], 0.0).then_inc(made, 1)
            gp.wait_ge(made, 1)
            nc.gpsimd.affine_select(out=ident[:], in_=ident[:], compare_op=ALU.not_equal, fill=1.0, base=0,
                                    pattern=[[-1, P]], channel_multiplier=1).then_inc(made, 1)

            def body(i, more):
                gp.wait_ge(var_done, i + 1)
                nc.gpsimd.tensor_tensor(rs[:, 1, :], rs[:, 0, :], power[:], ALU.pow).then_inc(rs_done, 1)

            over_blocks(gp, lambda i: None, body)

        @block.scalar
        def _(act):
            act.sem_inc(gelu_done, 2)
            nc.scalar.preload_act_table(ACT.Gelu)
            for r in range(NW):
                act.wait_ge(wt_full, r + 1)
                nc.scalar.activation(stage_target(r // 2, r % 2, table)[0], ps_t[r % 2][:].rearrange("p (k c) -> p k c", k=4),
                                     ACT.Copy).then_inc(wt_hi, 1)
            act.wait_ge(par, 32)

            def split_a(i):
                act.wait_ge(a_load, 16 * (i + 1))
                for k in range(OC):
                    if k == 0:
                        act.wait_ge(l3_full, 1 + OC * i)
                    nc.scalar.activation(a_hi[:, k, :], a_in[:, k, :], ACT.Copy).then_inc(ahi_done, 1)

            def body(i, more):
                for o in range(OC):
                    act.wait_ge(l3_full, 1 + OC * i + o + 1)
                    act.wait_ge(blo_done, 2 + OC * i + o - 1)
                    nc.scalar.activation(gelu[:, o % 2, :], ps_h[o % 2][:], ACT.Gelu, scale=scale[:, o:o + 1]).then_inc(gelu_done, 1)
                    act.wait_ge(gelu_done, 2 + OC * i + o + 1)
                    if o == 0:
                        act.wait_ge(l4_full, 1 + NT * i)
                    nc.scalar.activation(b_hi[:, o, :], gelu[:, o % 2, :], ACT.Copy).then_inc(bhi_done, 1)
                if more:
                    split_a(i + 1)

            over_blocks(act, split_a, body)

        @block.vector
        def _(dve):
            dve.sem_inc(alo_done, 1)
            dve.sem_inc(blo_done, 2)
            dve.sem_inc(l4_free, 2)
            dve.sem_inc(sum_done, 1)
            dve.sem_inc(out_done, 1)
            for r in range(NW):
                dve.wait_ge(wt_hi, r + 1)
                hi, lo = stage_target(r // 2, r % 2, table)
                nc.vector.tensor_tensor(lo, ps_t[r % 2][:].rearrange("p (k c) -> p k c", k=4), hi.bitcast(F32),
                                        ALU.subtract).then_inc(wt_free, 1)
            dve.wait_ge(par, 32)

            def split_a(i):
                for k in range(OC):
                    dve.wait_ge(ahi_done, OC * i + k + 1)
                    nc.vector.tensor_tensor(a_lo[:, k, :], a_in[:, k, :], a_hi[:, k, :].bitcast(F32), ALU.subtract).then_inc(alo_done, 1)

            def body(i, more):
                for o in range(OC):
                    dve.wait_ge(bhi_done, OC * i + o + 1)
                    nc.vector.tensor_tensor(b_lo[:, o, :], gelu[:, o % 2, :], b_hi[:, o, :].bitcast(F32), ALU.subtract).then_inc(blo_done, 1)
                if more:
                    split_a(i + 1)
                dve.wait_ge(x_load, 16 * (i + 1))
                dve.wait_ge(out_done, 1 + 16 * i)
                for t in range(NT):
                    dve.wait_ge(l4_full, 1 + NT * i + t + 1)
                    nc.vector.tensor_tensor(y[:, t, :], ps_o[t % 2][:, 0:C], scale_out[:], ALU.mult).then_inc(l4_free, 1)
                    dve.wait_ge(l4_free, 2 + NT * i + t + 1)
                    nc.vector.tensor_tensor(y[:, t, :], y[:, t, :], x_tok[:, t, :], ALU.add).then_inc(sum_done, 1)
                dve.wait_ge(sum_done, 1 + NT * (i + 1))
                for t in range(NT):
                    last = nc.vector.bn_stats(stats[:, t, :], y[:, t, :])
                last.then_inc(bn_done, 1)
                dve.wait_ge(bn_done, 2 * i + 1)
                nc.vector.memset(rs[:, 0, :], 1.0)
                for t in range(NT):
                    last = nc.vector.bn_aggr(mean_var[:, t, :], stats[:, t, :])
                last.then_inc(bn_done, 1)
                dve.wait_ge(bn_done, 2 * i + 2)
                nc.vector.tensor_scalar(rs[:, 0, :], mean_var[:, :, 1], EPS_LN, None, ALU.add).then_inc(var_done, 1)
                dve.wait_ge(rs_done, i + 1)
                for t in range(NT):
                    last = nc.vector.tensor_scalar(y[:, t, :], y[:, t, :], mean_var[:, t, 0:1], rs[:, 1, t:t + 1],
                                                   ALU.subtract, ALU.mult)
                last.then_inc(ln_done, 1)

            over_blocks(dve, split_a, body)

        @block.tensor
        def _(pe):
            pe.wait_ge(made, 2)
            pe.sem_inc(l3_full, 1)
            pe.sem_inc(l4_full, 1)
            for r in range(NW):
                pe.wait_ge(staged[(r // 2) % 2], 16 * (r // 4 + 1))
                if r >= 2:
                    pe.wait_ge(wt_free, r - 1)
                for q in range(4):
                    last = nc.tensor.transpose(ps_t[r % 2][:, q * P:(q + 1) * P],
                                               stage[(r // 2) % 2][:, (4 * (r % 2) + q) * P:(4 * (r % 2) + q + 1) * P], ident[:])
                last.then_inc(wt_full, 1)
            pe.wait_ge(wt_free, NW)

            def body(i, more):
                for o in range(OC):
                    col = slice(o * P, (o + 1) * P)
                    pe.wait_ge(gelu_done, 2 + OC * i + o - 1)
                    for k in range(OC):
                        if o == 0:
                            pe.wait_ge(alo_done, 1 + OC * i + k + 1)
                        for j, (w, p) in enumerate(((h2_hi, a_hi), (h2_lo, a_hi), (h2_hi, a_lo))):
                            last = nc.tensor.matmul(ps_h[o % 2][:], w[:, k, col], p[:, k, :], start=k == 0 and j == 0,
                                                    stop=k == OC - 1 and j == 2)
                    last.then_inc(l3_full, 1)
                for t in range(NT):
                    tok = slice(t * P, (t + 1) * P)
                    pe.wait_ge(l4_free, 2 + NT * i + t - 1)
                    for k in range(OC):
                        if t == 0:
                            pe.wait_ge(blo_done, 2 + OC * i + k + 1)
                        for j, (p, w) in enumerate(((b_hi, w3_hi), (b_hi, w3_lo), (b_lo, w3_hi))):
                            last = nc.tensor.matmul(ps_o[t % 2][:, 0:C], p[:, k, tok], w[:, k, :], start=k == 0 and j == 0,
                                                    stop=k == OC - 1 and j == 2)
                    last.then_inc(l4_full, 1)

            over_blocks(pe, lambda i: None, body)


def program(nc, a, out):
    x1 = nc.dram_tensor("x1", (B * T, C), F32, kind="Internal").ap()
    hidden = nc.dram_tensor("hidden", (HID, B * T), F32, kind="Internal").ap()
    attention(nc, a["L0_attn_x"], a["L0_attn_Wq"], a["L0_attn_Wk"], a["L0_attn_Wv"], a["L0_attn_Wproj"],
              a["L0_attn_q_rms_w"], a["L0_attn_k_rms_w"], a["L0_attn_omega"], a["L0_attn_u"], x1)
    ffn_up(nc, x1, a["L0_ffn_w1_w"], a["L0_ffn_w1_s"], a["L0_ffn_w2_w"], a["L0_ffn_w2_s"], a["L0_ffn_h1_w"],
           a["L0_ffn_h1_s"], hidden)
    ffn_down(nc, hidden, x1, a["L0_ffn_h2_w"], a["L0_ffn_h2_s"], a["L0_ffn_w3_w"], a["L0_ffn_w3_s"], out)


SHAPES = {"L0_attn_x": (B * T, C), "L0_attn_Wq": (C, H * D), "L0_attn_Wk": (C, H * D), "L0_attn_Wv": (C, H * D),
          "L0_attn_Wproj": (H * D, C), "L0_attn_q_rms_w": (D,), "L0_attn_k_rms_w": (D,), "L0_attn_omega": (H,),
          "L0_attn_u": (H, D), "L0_ffn_w1_w": (HID, C), "L0_ffn_w1_s": (HID,), "L0_ffn_w2_w": (HID, C),
          "L0_ffn_w2_s": (HID,), "L0_ffn_h1_w": (HID, HID), "L0_ffn_h1_s": (HID,), "L0_ffn_h2_w": (HID, HID),
          "L0_ffn_h2_s": (HID,), "L0_ffn_w3_w": (C, HID), "L0_ffn_w3_s": (C,)}


def kernel(**inputs):
    import numpy as _np
    import concourse.bacc as _bacc
    from concourse import mybir as _mybir
    from concourse.bass_utils import run_bass_kernel_spmd as _run

    nc = _bacc.Bacc("TRN2", target_bir_lowering=False, num_devices=1)
    arrays, aps = {}, {}
    for name, shape in SHAPES.items():
        a = _np.ascontiguousarray(inputs[name]).reshape(shape)
        arrays[f"in_{name}_dram"] = a
        aps[name] = nc.dram_tensor(f"in_{name}_dram", a.shape, _mybir.dt.from_np(a.dtype), kind="ExternalInput").ap()
    out = nc.dram_tensor("out_0_dram", (B * T, C), _mybir.dt.float32, kind="ExternalOutput").ap()
    program(nc, aps, out)
    r = _run(nc, [arrays], core_ids=[0])
    return r.results[0]["out_0_dram"].reshape(B, T, C)
```

```python
import concourse.bass as bass
from concourse import mybir
from contextlib import ExitStack

F32 = mybir.dt.float32
F32R = mybir.dt.float32r
ACT = mybir.ActivationFunctionType
ALU = mybir.AluOpType
AX = mybir.AxisListType

B, T, C = 2, 2048, 256
H, D = 16, 64
HID = 1024
P = 128
TT = T // P
KC = C // P
QB = 512
NQB = T // QB
TQ = QB // P
NEG = -1.0e30
EPS_RMS, EPS_U, EPS_LN = 1e-5, 1e-6, 1e-5

CQ, CK, CG, CV = 0, D, 2 * D, 2 * D + 1
WCOLS = 3 * D + 2
ONE = WCOLS - 1
R_BIAS, R_SHIFT = D, 96

UNITS = [(qb, kt) for qb in range(NQB) for kt in range(TQ * (qb + 1))]
MAXES = [(qt, kc) for qt in range(TT) for kc in range(qt // TQ + 1)]
NU, NM = len(UNITS), len(MAXES)
LAG = 2
LEAD = 5
PR = 4
NPJ = TT // 2
NTR = 2 * NQB + NQB
NYM = 3
NXT = TT // 2
PAIRS = H // 2
OUTS = NQB * NYM
SOFTPLUS_PARTS = 7
GATE_PARTS = SOFTPLUS_PARTS + 2
GATE = 23
IDENT_MADE = 2
GP_CONSTANTS = 20 + H + 2
BEFORE = 2 * NU


def group_end(qb):
    return sum(1 for qt, _ in MAXES if qt // TQ <= qb)


def segment_steps(main, turned, projected, more, odd, new_x):
    extra = []
    if turned:
        extra += [(0.0, ("values in",)), (0.0, ("bias",))]
        extra += [(0.01 + 0.045 * i, ("turn", i)) for i in range(2 * NQB)]
        last_turn = 0.01 + 0.045 * (2 * NQB - 1)
        for v, (qt, kc) in enumerate(MAXES):
            qb = qt // TQ
            at = max(0.10 + 0.84 * v / (NM - 1), 0.01 + 0.045 * (2 * qb + 1) + 0.02)
            extra.append((at, ("max", v)))
            if v + 1 == group_end(qb):
                extra.append((at, ("negmax", qb)))
                extra.append((max(at + 0.04, last_turn + 0.02 + 0.001 * qb), ("shift", qb)))
    if new_x:
        extra += [(0.005 + 0.028 * j, ("new x", j)) for j in range(NXT)]
    if projected:
        extra += [(0.26 + 0.025 * j, ("project", j)) for j in range(NPJ)]
        extra += [(0.47, ("square",)), (0.56, ("sumsq",)), (0.57, ("power",)), (0.71, ("gate a", 0)), (0.72, ("gate a", 1)), (0.73, ("gate exp",)),
                  (0.74, ("gate b", 0)), (0.76, ("gate b", 1))]
        extra += [(0.78 + 0.022 * i, ("gate c", i)) for i in range(GATE_PARTS)]
    if more:
        extra += [(0.60, ("weights",))]
    if main and not odd:
        extra += [(0.12, ("output weights",))]
    extra.sort(key=lambda e: e[0])
    length = [min(TQ, TQ * (qb + 1) - kt) for qb, kt in UNITS]
    steps, done, outs = [], 0, []

    def tile(name, u):
        if u < NU if main else u >= NU:
            steps.append((name, u % NU, not main))
        elif main and turned:
            steps.append((name, u - NU, True))

    if not main:
        steps = [step for _, step in extra]
        if not turned:
            return steps
    for u in range(LEAD if main else NU, NU + LEAD):
        tile("scores", u)
        tile("values", u - LAG)
        qb, kt = UNITS[(u - LAG) % NU]
        if main and u - LAG < NU and kt == TQ * (qb + 1) - 1:
            steps.append(("divide", qb))
            if odd:
                outs += [(u + 1 + i, ("out", qb, i)) for i in range(NYM)]
        done += length[u % NU]
        while outs and outs[0][0] <= u:
            steps.append(outs.pop(0)[1])
        while main and extra and (extra[0][0] * sum(length) <= done or u == NU + LEAD - 1):
            steps.append(extra.pop(0)[1])
    assert not outs
    return steps


def attention(nc, x, wq, wk, wv, wproj, q_rms_w, k_rms_w, omega, u, sum_dram):
    ctx = ExitStack()
    with ctx:
        def sb(name, shape, dt=F32):
            return ctx.enter_context(nc.sbuf_tensor(name, shape, dt))

        def pb(name):
            return ctx.enter_context(nc.psum_tensor(name, [P, 512], F32))

        def sem(name):
            return ctx.enter_context(nc.semaphore(name))

        ident = sb("ident", [P, P])
        ident_r = sb("ident_r", [P, P], F32R)
        mask_kq = sb("mask_kq", [P, P], F32R)
        mask_qk = sb("mask_qk", [P, P], F32R)
        mask_f = sb("mask_f", [P, 2, P])
        acc = sb("acc", [P, TT, C])
        xt_hi = sb("xt_hi", [P, KC, T], F32R)
        xt_lo = sb("xt_lo", [P, KC, T], F32R)
        w_in = sb("w_in", [P, KC, WCOLS])
        w_hi = sb("w_hi", [P, KC, WCOLS], F32R)
        w_lo = sb("w_lo", [P, KC, WCOLS], F32R)
        wg_tmp = sb("wg_tmp", [P, KC, D])
        raw = sb("raw", [P, TT, WCOLS])
        values = [sb(f"values{i}", [P, TT, D + 1]) for i in range(2)]
        x_rows = [sb(f"x_rows{i}", [P, 2, C]) for i in range(2)]
        k_tok = sb("k_tok", [P, TT, P])
        q_tok = sb("q_tok", [P, TT, P])
        k_split = [sb(f"k_split{i}", [P, T], F32R) for i in range(2)]
        q_twice = [sb(f"q_twice{i}", [P, T], F32R) for i in range(2)]
        k_ext = [sb(f"k_ext{i}", [P, T], F32R) for i in range(2)]
        q_ext = [sb(f"q_ext{i}", [P, T], F32R) for i in range(2)]
        q_max = [sb(f"q_max{i}", [P, T], F32R) for i in range(2)]
        bias = [sb(f"bias{i}", [P, TT, NQB]) for i in range(2)]
        away = sb("away", [P, TT, NQB])
        key_no = sb("key_no", [P, TT])
        exps = sb("exps", [P, PR, QB])
        y_tok = sb("y_tok", [P, TT, P])
        yt_hi = sb("yt_hi", [P, QB], F32R)
        yt_lo = sb("yt_lo", [P, QB], F32R)
        wp_in = sb("wp_in", [P, C])
        wp_hi = sb("wp_hi", [P, C], F32R)
        wp_lo = sb("wp_lo", [P, C], F32R)
        sumsq = sb("sumsq", [P, 2, TT])
        mean_sq = sb("mean_sq", [P, 2, TT])
        rs = sb("rs", [P, 2, TT])
        power = sb("power", [P, 2 * TT])
        g = sb("g", [P, 10, TT])
        c_hi = sb("c_hi", [P, TT], F32R)
        jc_hi = sb("jc_hi", [P, TT], F32R)
        maxes = sb("maxes", [P, TT, NQB])
        neg_max = sb("neg_max", [P, TT], F32R)
        recip = sb("recip", [P, TQ])
        omega_eff = sb("omega_eff", [P, H])
        slopes = sb("slopes", [P, H])
        u_gate = sb("u_gate", [P, H, D])
        u_norm = sb("u_norm", [P, 2, H])
        half = sb("half", [P, H])
        one = sb("one", [P, KC])
        qk_w = sb("qk_w", [P, D])
        rms_in = sb("rms_in", [P, 2, D])

        ps_s = [pb(f"ps_s{i}") for i in range(2)]
        ps_m = [pb(f"ps_m{i}") for i in range(2)]
        ps_v = pb("ps_v")
        ps_p = pb("ps_p")
        ps_t = pb("ps_t")
        ps_y = pb("ps_y")

        s_par = sem("s_par")
        s_cg = sem("s_cg")
        s_cv = sem("s_cv")
        s_ce = sem("s_ce")
        s_pw = sem("s_pw")
        s_const = sem("s_const")
        x_in = sem("x_in")
        xr_in = [sem(f"xr_in{i}") for i in range(2)]
        w_load = sem("w_load")
        v_in = sem("v_in")
        bias_done = sem("bias_done")
        wg_t = sem("wg_t")
        wg_done = sem("wg_done")
        w_done = sem("w_done")
        wp_load = sem("wp_load")
        wp_done = sem("wp_done")
        pj_full = sem("pj_full")
        pj_free = sem("pj_free")
        sq_done = sem("sq_done")
        ss_part = sem("ss_part")
        ms_done = sem("ms_done")
        rs_done = sem("rs_done")
        nrm = sem("nrm")
        gate = sem("gate")
        gate_e = sem("gate_e")
        tok_done = sem("tok_done")
        tr_full = sem("tr_full")
        tr_free = sem("tr_free")
        qk_hi = sem("qk_hi")
        dup = [[sem(f"dup{i}{qb}") for qb in range(NQB)] for i in range(2)]
        mx_full = sem("mx_full")
        mx_free = sem("mx_free")
        nm_done = sem("nm_done")
        st_full = sem("st_full")
        ex_done = sem("ex_done")
        pv_done = sem("pv_done")
        rc_done = sem("rc_done")
        y_done = sem("y_done")
        ym_full = sem("ym_full")
        ym_free = sem("ym_free")
        yt_done = sem("yt_done")
        sum_out = sem("sum_out")

        def first_bank(j):
            return (ps_y, ps_v)[j % 2]

        class Segment:

            def __init__(self, main, turned, projected, h_projected, w, h_w, slot, pair=-1, hp=0, ym=0, yt=0, ym_last=0, new_x=False, batch=0):
                self.main, self.turned, self.projected, self.h_projected = main, turned, projected, h_projected
                self.w, self.h_w, self.slot, self.other = w, h_w, slot, 1 - slot
                self.pair, self.hp, self.ym, self.yt, self.ym_last, self.new_x = pair, hp, ym, yt, ym_last, new_x
                self.batch = batch
                self.steps = segment_steps(main is not None, turned is not None, projected is not None,
                                           w is not None, slot == 1, new_x)

            def attended(self, ahead):
                return (self.turned, self.other, self.pair + self.slot) if ahead else (self.main, self.slot, self.pair)

        def over_heads(eng, begin, segment, end):
            begin()
            segment(Segment(None, None, 0, 0, 1, 1, 1))
            segment(Segment(None, 0, 1, 1, 2, 2, 1))

            def pair_of(first, hp, batch):
                g = 2 * (first + hp)
                ym = NXT * (batch + 1) + OUTS * (first + hp)
                yt = NXT * (batch + 1) + NQB * (first + hp)
                h = 2 * hp
                segment(Segment(g, g + 1, g + 2, h + 2, g + 3, h + 3, 0, first + hp, hp, ym, yt, ym, batch=batch))
                return g, h, ym, yt

            for batch in range(B):
                first = batch * PAIRS
                with eng.Fori(0, PAIRS - 2) as hp:
                    g, h, ym, yt = pair_of(first, hp, batch)
                    segment(Segment(g + 1, g + 2, g + 3, h + 3, g + 4, h + 4, 1, first + hp, hp, ym, yt, ym, batch=batch))
                hp = PAIRS - 2
                g, h, ym, yt = pair_of(first, hp, batch)
                more = batch + 1 < B
                segment(Segment(g + 1, g + 2, g + 3, h + 3, g + 4 if more else None, 0, 1, first + hp, hp, ym, yt, ym, batch=batch))
                hp = PAIRS - 1
                g, ym, yt = g + 2, ym + OUTS, yt + NQB
                if more:
                    segment(Segment(g, g + 1, g + 2, 0, g + 3, 1, 0, first + hp, hp, ym + NXT, yt + NXT, ym, new_x=True, batch=batch))
                    segment(Segment(g + 1, g + 2, g + 3, 1, g + 4, 2, 1, first + hp, hp, ym + NXT, yt + NXT, ym, batch=batch))
                else:
                    segment(Segment(g, g + 1, None, 0, None, 0, 0, first + hp, hp, ym, yt, ym, batch=batch))
                    segment(Segment(g + 1, None, None, 0, None, 0, 1, first + hp, hp, ym, yt, ym, batch=batch))
                end(batch)

        block = ctx.enter_context(nc.Block())

        @block.sync
        def _(sp):
            for w, src in ((rms_in[:, 0, :], q_rms_w), (rms_in[:, 1, :], k_rms_w), (omega_eff[:], omega),
                           (u_gate[:].rearrange("p h d -> p (h d)"), u.rearrange("h d -> (h d)"))):
                sp.dma_start(w, src.partition_broadcast(P)).then_inc(s_par, 16)

            def load_weights(n, h):
                sp.wait_ge(w_done, 1 + 2 * n)
                for dst, src in ((CQ, wq), (CK, wk), (CV, wv)):
                    sp.dma_start(w_in[:, :, dst:dst + D],
                                 src[:, bass.ds(h * D, D)].rearrange("(k p) d -> p k d", p=P)).then_inc(w_load, 16)

            def load_x_rows(batch, ym, j):
                if j >= 2:
                    sp.wait_ge(ym_full, 1 + ym + j - 1)
                row = batch * T + 2 * j * P
                sp.dma_start(x_rows[j % 2][:], x[row:row + 2 * P, :].rearrange("(t p) c -> p t c", p=P)).then_inc(xr_in[j % 2], 16)

            def load_acc(batch):
                sp.dma_start(acc[:], x[batch * T:(batch + 1) * T, :].rearrange("(t p) c -> p t c", p=P)).then_inc(x_in, 16)

            def begin():
                load_weights(0, 0)
                for j in range(NXT):
                    load_x_rows(0, 0, j)
                load_acc(0)

            def segment(sg):
                if sg.main is not None and sg.slot == 0:
                    sp.wait_ge(wp_done, 1 + 2 * sg.pair)
                    sp.dma_start(wp_in[:], wproj[bass.ds(sg.hp * P, P), :]).then_inc(wp_load, 16)
                if sg.new_x:
                    for j in range(NXT):
                        load_x_rows(1, sg.ym - NXT, j)
                for qc in range(NQB):
                    if sg.turned is not None:
                        n, s = sg.turned, sg.other
                        cols = slice(qc * QB, (qc + 1) * QB)
                        sp.wait_ge(qk_hi, 1 + 2 * NQB * n + 2 * qc + 1)
                        sp.dma_start(k_split[s][0:D, cols].bitcast(F32), k_ext[s][0:D, cols].bitcast(F32)).then_inc(dup[s][qc], 16)
                        sp.wait_ge(qk_hi, 1 + 2 * NQB * n + 2 * qc + 2)
                        sp.dma_start(q_twice[s][0:D, cols].bitcast(F32), q_max[s][0:D, cols].bitcast(F32)).then_inc(dup[s][qc], 16)
                        sp.dma_start(q_twice[s][D:P, cols].bitcast(F32), q_max[s][0:D, cols].bitcast(F32)).then_inc(dup[s][qc], 16)
                if sg.w is not None:
                    load_weights(sg.w, sg.h_w)

            def end(batch):
                for qb in range(NQB):
                    sp.wait_ge(ym_free, 1 + NXT * B + OUTS * PAIRS * (batch + 1) - NYM * (NQB - 1 - qb))
                    sp.dma_start(sum_dram[batch * T + qb * QB:batch * T + (qb + 1) * QB, :].rearrange("(t p) c -> p t c", p=P),
                                 acc[:, qb * TQ:(qb + 1) * TQ, :]).then_inc(sum_out, 16)
                sp.wait_ge(sum_out, 16 * NQB * (batch + 1))
                if batch + 1 < B:
                    load_acc(batch + 1)

            over_heads(sp, begin, segment, end)

        @block.gpsimd
        def _(gp):
            made = [0]

            def link(ins):
                made[0] += 1
                ins.then_inc(s_cg, 1)
                gp.wait_ge(s_cg, made[0])

            gp.sem_inc(w_done, 1)
            gp.sem_inc(wp_done, 1)
            link(nc.gpsimd.memset(ident[:], 0.0))
            link(nc.gpsimd.affine_select(out=ident[:], in_=ident[:], compare_op=ALU.not_equal, fill=1.0, base=0,
                                        pattern=[[-1, P]], channel_multiplier=1))
            assert made[0] == IDENT_MADE
            link(nc.gpsimd.memset(mask_f[:], 0.0))
            link(nc.gpsimd.memset(k_tok[:], 0.0))
            link(nc.gpsimd.memset(q_tok[:], 0.0))
            link(nc.gpsimd.memset(y_tok[:], 0.0))
            link(nc.gpsimd.memset(power[:], -0.5))
            link(nc.gpsimd.memset(half[:], 0.5))
            link(nc.gpsimd.memset(one[:], 1.0))
            for i in range(2):
                link(nc.gpsimd.memset(values[i][:, :, D:D + 1], 1.0))
            link(nc.gpsimd.memset(w_in[:, :, CG:CG + 1], 0.0))
            link(nc.gpsimd.memset(w_in[:, :, ONE:ONE + 1], 0.0))
            for h in range(H):
                link(nc.gpsimd.memset(slopes[:, h:h + 1], 2.0 ** (-0.5 * (h + 1))))
            link(nc.gpsimd.affine_select(out=mask_f[:, 0, :], in_=mask_f[:, 0, :], compare_op=ALU.is_ge, fill=NEG,
                                        base=0, pattern=[[1, P]], channel_multiplier=-1))
            link(nc.gpsimd.affine_select(out=mask_f[:, 1, :], in_=mask_f[:, 1, :], compare_op=ALU.is_ge, fill=NEG,
                                        base=0, pattern=[[-1, P]], channel_multiplier=1))
            link(nc.gpsimd.memset(k_tok[:, :, R_SHIFT:R_SHIFT + 1], 1.0))
            for r in range(2):
                link(nc.gpsimd.iota(q_tok[:, :, R_BIAS + r:R_BIAS + r + 1], pattern=[[-P, TT], [0, 1]], base=0,
                                   channel_multiplier=-1, allow_small_or_imprecise_dtypes=True))
            link(nc.gpsimd.memset(q_tok[:, :, R_BIAS + 2:R_BIAS + 4], 1.0))
            link(nc.gpsimd.iota(key_no[:], pattern=[[P, TT]], base=0, channel_multiplier=1,
                               allow_small_or_imprecise_dtypes=True))
            link(nc.gpsimd.iota(away[:], pattern=[[P, TT], [-QB, NQB]], base=0, channel_multiplier=1,
                               allow_small_or_imprecise_dtypes=True))
            ytok_rows = y_tok[:].rearrange("p t c -> p (t c)")
            link(nc.gpsimd.iota(ytok_rows[D:D + 2, :], pattern=[[0, NQB], [-1, QB]], base=0, channel_multiplier=0,
                               allow_small_or_imprecise_dtypes=True))
            assert made[0] == GP_CONSTANTS
            gp.wait_ge(s_cv, 2)
            nc.gpsimd.tensor_tensor(u_norm[:, 1, :], u_norm[:, 0, :], half[:], ALU.pow).then_inc(s_pw, 1)


            def split_weights(n):
                gp.wait_ge(w_load, 48 * (n + 1))
                gp.wait_ge(wg_done, n + 2)
                gp.wait_ge(pj_full, 1 + NPJ * n)
                nc.gpsimd.tensor_tensor(w_hi[:], w_in[:], one[:].unsqueeze(2).broadcast_to([P, KC, WCOLS]), ALU.mult).then_inc(w_done, 1)
                gp.wait_ge(w_done, 1 + 2 * n + 1)
                nc.gpsimd.tensor_tensor(w_lo[:], w_in[:], w_hi[:].bitcast(F32), ALU.subtract).then_inc(w_done, 1)

            def begin():
                split_weights(0)

            def segment(sg):
                for step in sg.steps:
                    if step[0] == "weights":
                        split_weights(sg.w)
                    if step[0] == "values in":
                        n = sg.turned
                        gp.wait_ge(pj_free, 1 + NPJ * (n + 1))
                        gp.wait_ge(pv_done, BEFORE + NU * (n - 1))
                        nc.gpsimd.tensor_tensor(values[sg.other][:, :, 0:D], raw[:, :, CV:CV + D],
                                                one[:, 0:1].unsqueeze(2).broadcast_to([P, TT, D]), ALU.mult).then_inc(v_in, 1)
                    if step[0] == "square":
                        n = sg.projected
                        gp.wait_ge(pj_free, 1 + NPJ * (n + 1))
                        if sg.turned is not None:
                            gp.wait_ge(tr_free, 1 + NTR * sg.turned + 2 * NQB)
                        nc.gpsimd.tensor_tensor(k_tok[:, :, 0:D], raw[:, :, CK:CK + D], raw[:, :, CK:CK + D], ALU.mult)
                        nc.gpsimd.tensor_tensor(q_tok[:, :, 0:D], raw[:, :, CQ:CQ + D], raw[:, :, CQ:CQ + D], ALU.mult).then_inc(sq_done, 1)
                    if step[0] == "power":
                        n = sg.projected
                        gp.wait_ge(ms_done, n + 2)
                        nc.gpsimd.tensor_tensor(rs[:].rearrange("p a t -> p (a t)"),
                                                mean_sq[:].rearrange("p a t -> p (a t)"), power[:],
                                                ALU.pow).then_inc(rs_done, 1)
                    if step[0] == "output weights":
                        gp.wait_ge(wp_load, 16 * (sg.pair + 1))
                        gp.wait_ge(ym_full, 1 + sg.ym_last)
                        nc.gpsimd.tensor_tensor(wp_hi[:], wp_in[:], one[:, 0:1].broadcast_to([P, C]), ALU.mult).then_inc(wp_done, 1)
                        gp.wait_ge(wp_done, 1 + 2 * sg.pair + 1)
                        nc.gpsimd.tensor_tensor(wp_lo[:], wp_in[:], wp_hi[:].bitcast(F32), ALU.subtract).then_inc(wp_done, 1)

            over_heads(gp, begin, segment, lambda batch: None)

        @block.scalar
        def _(act):
            nc.scalar.preload_act_table(ACT.Exp)
            act.sem_inc(pj_free, 1)
            act.sem_inc(v_in, 1)
            act.sem_inc(qk_hi, 1)
            act.sem_inc(ex_done, BEFORE)

            def turn_x(j, ym, bank=ps_y):
                act.wait_ge(ym_full, 1 + ym + j + 1)
                nc.scalar.activation(xt_hi[:, :, j * 2 * P:(j + 1) * 2 * P],
                                     bank[:].rearrange("p (k t) -> p k t", k=KC), ACT.Copy).then_inc(yt_done, 1)

            def begin():
                for j in range(NXT):
                    turn_x(j, 0, first_bank(j))
                act.wait_ge(s_cv, 4)
                nc.scalar.activation(g[:, 1, :], g[:, 0, :], ACT.Exp).then_inc(s_ce, 1)

            def segment(sg):
                for step in sg.steps:
                    if step[0] == "scores":
                        u_ = step[1]
                        n, slot, _ = sg.attended(step[2])
                        qb, kt = UNITS[u_]
                        off = max(0, kt - TQ * qb) * P
                        act.wait_ge(st_full, NU * n + u_ + 1)
                        act.wait_ge(pv_done, BEFORE + NU * n + u_ + 1 - PR)
                        nc.scalar.activation(exps[:, u_ % PR, off:QB], ps_s[u_ % 2][:, off:QB], ACT.Exp,
                                             bias=bias[slot][:, kt, qb:qb + 1]).then_inc(ex_done, 1)
                    if step[0] == "new x":
                        turn_x(step[1], sg.ym - NXT)
                    if step[0] == "project":
                        m, j = sg.projected, step[1]
                        act.wait_ge(pj_full, 1 + NPJ * m + j + 1)
                        if j == 0:
                            act.wait_ge(gate, 1 + GATE * m)
                            act.wait_ge(v_in, 1 + m)
                        nc.scalar.activation(raw[:, 2 * j:2 * j + 2, 0:ONE],
                                             ps_p[:, 0:2 * WCOLS].rearrange("p (t c) -> p t c", t=2)[:, :, 0:ONE],
                                             ACT.Copy).then_inc(pj_free, 1)
                    if step[0] == "gate exp":
                        act.wait_ge(gate, 1 + GATE * sg.projected + 2)
                        nc.scalar.activation(g[:, 1, :], g[:, 0, :], ACT.Exp).then_inc(gate_e, 1)
                    if step[0] == "turn":
                        m, i = sg.turned, step[1]
                        cols = slice((i // 2) * QB, (i // 2 + 1) * QB)
                        dst = (k_ext, q_max)[i % 2][sg.other]
                        act.wait_ge(tr_full, 1 + NTR * m + i + 1)
                        nc.scalar.activation(dst[:, cols], ps_t[:], ACT.Copy).then_inc(qk_hi, 1)
                    if step[0] == "out" and step[2] == 0:
                        qb = step[1]
                        act.wait_ge(ym_full, 1 + sg.ym + NYM * qb + 1)
                        nc.scalar.activation(yt_hi[:], ps_y[:], ACT.Copy).then_inc(yt_done, 1)

            over_heads(act, begin, segment, lambda batch: None)

        @block.vector
        def _(dve):
            def softplus(link, x_ap, out_ap, part):
                e, s, z, p, r = (g[:, i, :] for i in (1, 2, 3, 4, 5))
                if part == 0:
                    link(nc.vector.tensor_scalar(s, e, 2.0, None, ALU.add))
                    link(nc.vector.reciprocal(r, s))
                if part == 1:
                    link(nc.vector.tensor_tensor(s, e, r, ALU.mult))
                    link(nc.vector.tensor_tensor(z, s, s, ALU.mult))
                if part == 2:
                    link(nc.vector.tensor_scalar(p, z, 1.0 / 15, None, ALU.mult))
                for k in {2: (13,), 3: (11, 9), 4: (7, 5), 5: (3,)}.get(part, ()):
                    link(nc.vector.scalar_tensor_tensor(p, p, 1.0 / k, z, ALU.add, ALU.mult))
                if part == 5:
                    link(nc.vector.scalar_tensor_tensor(p, p, 1.0, s, ALU.add, ALU.mult))
                if part == 6:
                    link(nc.vector.tensor_scalar(r, x_ap, 0.0, None, ALU.max))
                    link(nc.vector.scalar_tensor_tensor(out_ap, p, 2.0, r, ALU.mult, ALU.add))

            def turn_x(j, yt, bank=ps_y):
                dve.wait_ge(yt_done, yt + j + 1)
                cols = slice(j * 2 * P, (j + 1) * 2 * P)
                nc.vector.tensor_tensor(xt_lo[:, :, cols], bank[:].rearrange("p (k t) -> p k t", k=KC),
                                        xt_hi[:, :, cols].bitcast(F32), ALU.subtract).then_inc(ym_free, 1)

            dve.sem_inc(ym_free, 1)
            for j in range(NXT):
                turn_x(j, 0, first_bank(j))

            count = [0]

            def link(ins):
                count[0] += 1
                ins.then_inc(s_cv, 1)
                dve.wait_ge(s_cv, count[0])

            dve.wait_ge(s_par, 64)
            dve.wait_ge(s_cg, GP_CONSTANTS)
            link(nc.vector.tensor_tensor(exps[:, 0:2, :].rearrange("p a (h d) -> p (a h) d", d=D), u_gate[:], u_gate[:], ALU.mult))
            link(nc.vector.tensor_reduce(u_norm[:, 0, :], exps[:, 0:2, :].rearrange("p a (h d) -> p (a h) d", d=D), AX.X, ALU.add))
            link(nc.vector.tensor_scalar(g[:, 6, :], omega_eff[:], 0.0, None, ALU.add))
            link(nc.vector.scalar_tensor_tensor(g[:, 0, :], g[:, 6, :], -1.0, g[:, 6, :], ALU.mult, ALU.min))
            dve.wait_ge(s_ce, 1)
            for part in range(SOFTPLUS_PARTS):
                softplus(link, g[:, 6, :], g[:, 7, :], part)
            link(nc.vector.tensor_tensor(omega_eff[:], g[:, 7, :], slopes[:], ALU.mult))
            dve.wait_ge(s_pw, 1)
            link(nc.vector.tensor_scalar(u_norm[:, 0, :], u_norm[:, 1, :], EPS_U, None, ALU.max))
            link(nc.vector.reciprocal(u_norm[:, 1, :], u_norm[:, 0, :]))
            link(nc.vector.tensor_tensor(u_gate[:], u_gate[:], u_norm[:, 1, :].unsqueeze(2).broadcast_to([P, H, D]), ALU.mult))
            link(nc.vector.tensor_scalar(rms_in[:, 1, :], rms_in[:, 1, :], D ** -0.5, None, ALU.mult))
            link(nc.vector.tensor_tensor(u_gate[:], u_gate[:], rms_in[:, 1:2, :].broadcast_to([P, H, D]), ALU.mult))
            link(nc.vector.tensor_tensor(qk_w[:], rms_in[:, 0, :], rms_in[:, 1, :], ALU.mult))
            nc.vector.tensor_copy(ident_r[:], ident[:])
            nc.vector.tensor_copy(mask_kq[:], mask_f[:, 0, :])
            nc.vector.tensor_copy(mask_qk[:], mask_f[:, 1, :])
            rows = y_tok[:].rearrange("p t c -> p (t c)")
            for i in range(2):
                link(nc.vector.tensor_copy(q_ext[i][D:P, :], q_tok[D:P, :, R_BIAS + 4:R_BIAS + 5].broadcast_to([D, TT, P])))
                link(nc.vector.tensor_copy(q_ext[i][D:D + 2, :], rows[D:D + 2, :]))
            nc.vector.memset(mean_sq[:], 1.0).then_inc(s_const, 1)
            dve.sem_inc(wg_done, 1)
            dve.sem_inc(ms_done, 1)
            dve.sem_inc(gate, 1)
            dve.sem_inc(tr_free, 1)
            dve.sem_inc(mx_free, 2)
            dve.sem_inc(nm_done, 1)
            dve.sem_inc(y_done, 1)
            dve.sem_inc(nrm, 1)
            dve.wait_ge(s_const, 1)

            def gate_weights(n, h):
                dve.wait_ge(w_load, 48 * (n + 1))
                dve.wait_ge(wg_done, n + 1)
                nc.vector.tensor_tensor(wg_tmp[:], w_in[:, :, CK:CK + D],
                                        u_gate[:, bass.ds(h, 1), :].broadcast_to([P, KC, D]), ALU.mult).then_inc(wg_t, 1)
                dve.wait_ge(wg_t, n + 1)
                nc.vector.tensor_reduce(w_in[:, :, CG:CG + 1], wg_tmp[:], AX.X, ALU.add).then_inc(wg_done, 1)

            def begin():
                gate_weights(0, 0)

            def segment(sg):
                n, second = sg.main, sg.slot
                m, s = sg.turned, sg.other
                gcount = [0]

                def glink(ins):
                    gcount[0] += 1
                    ins.then_inc(gate, 1)
                    dve.wait_ge(gate, 1 + GATE * sg.projected + gcount[0])

                for step in sg.steps:
                    if step[0] == "weights":
                        gate_weights(sg.w, sg.h_w)
                    if step[0] == "new x":
                        turn_x(step[1], sg.yt - NXT)
                    if step[0] == "bias":
                        dve.wait_ge(gate, 1 + GATE * (m + 1))
                        dve.wait_ge(ex_done, BEFORE + NU * (m - 1))
                        nc.vector.tensor_tensor(bias[s][:], away[:], k_tok[:, :, R_BIAS:R_BIAS + 1].broadcast_to([P, TT, NQB]),
                                                ALU.mult).then_inc(bias_done, 1)
                    if step[0] == "sumsq":
                        dve.wait_ge(sq_done, sg.projected + 1)
                        nc.vector.tensor_reduce(sumsq[:, 0, :], k_tok[:, :, 0:D], AX.X, ALU.add)
                        nc.vector.tensor_reduce(sumsq[:, 1, :], q_tok[:, :, 0:D], AX.X, ALU.add).then_inc(ss_part, 1)
                        dve.wait_ge(ss_part, sg.projected + 1)
                        nc.vector.tensor_scalar(mean_sq[:], sumsq[:], 1.0 / D, EPS_RMS, ALU.mult, ALU.add).then_inc(ms_done, 1)
                    if step == ("gate a", 0):
                        dve.wait_ge(rs_done, sg.projected + 1)
                        glink(nc.vector.tensor_tensor(g[:, 6, :], raw[:, :, CG], rs[:, 0, :], ALU.mult))
                        glink(nc.vector.scalar_tensor_tensor(g[:, 0, :], g[:, 6, :], -1.0, g[:, 6, :], ALU.mult, ALU.min))
                    if step == ("gate a", 1):
                        glink(nc.vector.tensor_tensor(q_tok[:, :, 0:D], raw[:, :, CQ:CQ + D],
                                                      rs[:, 1, :].unsqueeze(2).broadcast_to([P, TT, D]), ALU.mult))
                    if step == ("gate b", 0):
                        glink(nc.vector.tensor_tensor(k_tok[:, :, 0:D], raw[:, :, CK:CK + D],
                                                      rs[:, 0, :].unsqueeze(2).broadcast_to([P, TT, D]), ALU.mult))
                    if step == ("gate b", 1):
                        glink(nc.vector.tensor_tensor(q_tok[:, :, 0:D], q_tok[:, :, 0:D],
                                                      qk_w[:].unsqueeze(1).broadcast_to([P, TT, D]), ALU.mult))
                    c, jc = k_tok[:, :, R_BIAS], k_tok[:, :, R_BIAS + 2]
                    if step[0] == "gate c" and step[1] < SOFTPLUS_PARTS:
                        if step[1] == 0:
                            dve.wait_ge(gate_e, sg.projected + 1)
                        softplus(glink, g[:, 6, :], g[:, 7, :], step[1])
                    if step == ("gate c", SOFTPLUS_PARTS):
                        glink(nc.vector.tensor_scalar(c, g[:, 7, :], omega_eff[:, bass.ds(sg.h_projected, 1)], None, ALU.mult))
                        glink(nc.vector.tensor_tensor(jc, c, key_no[:], ALU.mult))
                    if step == ("gate c", SOFTPLUS_PARTS + 1):
                        nc.vector.tensor_copy(c_hi[:], c)
                        glink(nc.vector.tensor_copy(jc_hi[:], jc))
                        nc.vector.tensor_tensor(k_tok[:, :, R_BIAS + 1], c, c_hi[:].bitcast(F32), ALU.subtract)
                        glink(nc.vector.tensor_tensor(k_tok[:, :, R_BIAS + 3], jc, jc_hi[:].bitcast(F32), ALU.subtract))
                        assert gcount[0] == GATE
                    if step[0] == "turn":
                        i = step[1]
                        cols = slice((i // 2) * QB, (i // 2 + 1) * QB)
                        dve.wait_ge(qk_hi, 1 + 2 * NQB * m + i + 1)
                        dst, hi = ((k_split[s][D:P, cols], k_ext[s]), (q_ext[s][0:D, cols], q_max[s]))[i % 2]
                        nc.vector.tensor_tensor(dst, ps_t[0:D, :], hi[0:D, cols].bitcast(F32), ALU.subtract).then_inc(tr_free, 1)
                    if step[0] == "max":
                        v = step[1]
                        qt, kc = MAXES[v]
                        width = min(QB, (qt + 1) * P - kc * QB)
                        dve.wait_ge(mx_full, NM * m + v + 1)
                        if v == 0:
                            dve.wait_ge(nm_done, 1 + NQB * m)
                        nc.vector.tensor_reduce(maxes[:, qt, kc:kc + 1], ps_m[v % 2][:, 0:width], AX.X, ALU.max).then_inc(mx_free, 1)
                    if step[0] == "negmax":
                        qb = step[1]
                        dve.wait_ge(mx_free, 2 + NM * m + group_end(qb))
                        nc.vector.tensor_reduce(neg_max[:, qb * TQ:(qb + 1) * TQ], maxes[:, qb * TQ:(qb + 1) * TQ, 0:qb + 1],
                                                AX.X, ALU.max, negate=True).then_inc(nm_done, 1)
                    if step[0] == "shift":
                        qb = step[1]
                        dve.wait_ge(tr_full, 1 + NTR * m + 2 * NQB + qb + 1)
                        nc.vector.tensor_copy(q_ext[s][R_SHIFT:R_SHIFT + 1, qb * QB:(qb + 1) * QB],
                                              ps_t[R_SHIFT:R_SHIFT + 1, :]).then_inc(tr_free, 1)
                    if step[0] == "divide":
                        qb = step[1]
                        pv = ps_v[:, 0:TQ * (D + 1)].rearrange("p (t c) -> p t c", t=TQ)
                        dve.wait_ge(pv_done, BEFORE + NU * n + len([1 for q, _ in UNITS if q <= qb]))
                        dve.wait_ge(y_done, 1 + NQB * n + qb)
                        nc.vector.reciprocal(recip[:], pv[:, :, D]).then_inc(rc_done, 1)
                        dve.wait_ge(rc_done, NQB * n + qb + 1)
                        nc.vector.tensor_tensor(y_tok[:, qb * TQ:(qb + 1) * TQ, second * D:(second + 1) * D],
                                                pv[:, :, 0:D], recip[:].unsqueeze(2).broadcast_to([P, TQ, D]), ALU.mult).then_inc(y_done, 1)
                    if step[0] == "out":
                        qb, i = step[1], step[2]
                        if i == 0:
                            dve.wait_ge(yt_done, sg.yt + qb + 1)
                            nc.vector.tensor_tensor(yt_lo[:], ps_y[:], yt_hi[:].bitcast(F32), ALU.subtract).then_inc(ym_free, 1)
                        else:
                            t0 = qb * TQ + 2 * (i - 1)
                            if qb == 0 and i == 1:
                                dve.wait_ge(x_in, 16 * (sg.batch + 1))
                            dve.wait_ge(ym_full, 1 + sg.ym + NYM * qb + i + 1)
                            nc.vector.tensor_tensor(acc[:, t0:t0 + 2, :], acc[:, t0:t0 + 2, :],
                                                    ps_y[:].rearrange("p (t c) -> p t c", t=2), ALU.add).then_inc(ym_free, 1)

            over_heads(dve, begin, segment, lambda batch: None)

        @block.tensor
        def _(pe):
            pe.wait_ge(s_cg, IDENT_MADE)
            pe.sem_inc(pj_full, 1)
            pe.sem_inc(tr_full, 1)
            pe.sem_inc(ym_full, 1)
            pe.sem_inc(pv_done, BEFORE)

            def turn_x(j, ym, batch):
                pe.wait_ge(xr_in[j % 2], 16 * (NXT // 2 * batch + j // 2 + 1))
                pe.wait_ge(ym_free, 1 + ym + (max(0, j - 1) if batch == 0 else j))
                bank = first_bank(j) if batch == 0 else ps_y
                for k in range(KC):
                    for t in range(2):
                        last = nc.tensor.transpose(bank[:, (2 * k + t) * P:(2 * k + t + 1) * P],
                                                   x_rows[j % 2][:, t, k * P:(k + 1) * P], ident[:])
                last.then_inc(ym_full, 1)

            def begin():
                for j in range(NXT):
                    turn_x(j, 0, 0)
                pe.wait_ge(s_const, 1)

            def split_product(out, pairs):
                terms = [(a, c) for (ah, al), (ch, cl) in pairs for a, c in ((ah, ch), (ah, cl), (al, ch))]
                for i, (a, c) in enumerate(terms):
                    last = nc.tensor.matmul(out, a, c, start=i == 0, stop=i == len(terms) - 1)
                return last

            def segment(sg):
                m, s = sg.turned, sg.other
                for step in sg.steps:
                    if step[0] == "new x":
                        turn_x(step[1], sg.ym - NXT, 1)
                    if step[0] == "scores":
                        u_ = step[1]
                        n, second, pair = sg.attended(step[2])
                        qb, kt = UNITS[u_]
                        diag = kt >= TQ * qb
                        off = max(0, kt - TQ * qb) * P
                        if kt == 0:
                            pe.wait_ge(tr_free, 1 + NTR * n + 2 * NQB + qb + 1)
                            pe.wait_ge(dup[second][qb], 48 * (pair + 1))
                        if u_ == 0:
                            pe.wait_ge(v_in, 1 + n + 1)
                            pe.wait_ge(bias_done, n + 1)
                        pe.wait_ge(ex_done, BEFORE + NU * n + u_ + 1 - 2)
                        out = ps_s[u_ % 2][:, off:QB]
                        q = slice(qb * QB + off, (qb + 1) * QB)
                        k = slice(kt * P, (kt + 1) * P)
                        nc.tensor.matmul(out, k_split[second][:, k], q_twice[second][:, q], start=True, stop=False)
                        last = nc.tensor.matmul(out, k_ext[second][:, k], q_ext[second][:, q], start=False, stop=not diag)
                        if diag:
                            last = nc.tensor.matmul(ps_s[u_ % 2][:, off:off + P], ident_r[:], mask_kq[:], start=False, stop=True)
                        last.then_inc(st_full, 1)
                    if step[0] == "values":
                        u_ = step[1]
                        n, second, _ = sg.attended(step[2])
                        qb, kt = UNITS[u_]
                        pe.wait_ge(ex_done, BEFORE + NU * n + u_ + 1)
                        if kt == 0:
                            pe.wait_ge(y_done, 1 + NQB * n + qb)
                        for t in range(max(0, kt - TQ * qb), TQ):
                            last = nc.tensor.matmul(ps_v[:, t * (D + 1):(t + 1) * (D + 1)],
                                                    exps[:, u_ % PR, t * P:(t + 1) * P],
                                                    values[second][:, kt, :],
                                                    start=(kt == 0 and t == 0), stop=(kt == TQ * qb + t),
                                                    skip_group_check=True)
                        last.then_inc(pv_done, 1)
                    if step[0] == "project":
                        j, p = step[1], sg.projected
                        if j == 0:
                            pe.wait_ge(w_done, 1 + 2 * (p + 1))
                            pe.wait_ge(ym_free, 1 + NXT)
                            if sg.new_x:
                                pe.wait_ge(ym_free, 1 + sg.ym)
                        pe.wait_ge(pj_free, 1 + NPJ * p + j)
                        for t in range(2):
                            tok = slice((2 * j + t) * P, (2 * j + t + 1) * P)
                            last = split_product(ps_p[:, t * WCOLS:(t + 1) * WCOLS],
                                                 [((xt_hi[:, k, tok], xt_lo[:, k, tok]), (w_hi[:, k, :], w_lo[:, k, :]))
                                                  for k in range(KC)])
                        last.then_inc(pj_full, 1)
                    if step[0] == "turn":
                        i = step[1]
                        if i == 0:
                            pe.wait_ge(gate, 1 + GATE * (m + 1))
                        pe.wait_ge(tr_free, 1 + NTR * m + i)
                        src = (k_tok, q_tok)[i % 2]
                        for t in range(TQ):
                            last = nc.tensor.transpose(ps_t[:, t * P:(t + 1) * P], src[:, (i // 2) * TQ + t, :], ident[:])
                        last.then_inc(tr_full, 1)
                    if step[0] == "max":
                        v = step[1]
                        qt, kc = MAXES[v]
                        if kc == 0 and qt % TQ == 0:
                            pe.wait_ge(qk_hi, 1 + 2 * NQB * m + 2 * (qt // TQ) + 2)
                        pe.wait_ge(mx_free, 2 + NM * m + v + 1 - 2)
                        width = min(QB, (qt + 1) * P - kc * QB)
                        diag = kc == qt // TQ
                        last = nc.tensor.matmul(ps_m[v % 2][:, 0:width], q_max[s][:, qt * P:(qt + 1) * P],
                                                k_ext[s][:, kc * QB:kc * QB + width], start=True, stop=not diag)
                        if diag:
                            last = nc.tensor.matmul(ps_m[v % 2][:, width - P:width], ident_r[:], mask_qk[:], start=False, stop=True)
                        last.then_inc(mx_full, 1)
                    if step[0] == "shift":
                        qb = step[1]
                        pe.wait_ge(nm_done, 1 + NQB * m + qb + 1)
                        pe.wait_ge(tr_free, 1 + NTR * m + 2 * NQB + qb)
                        for t in range(TQ):
                            col = neg_max[:, qb * TQ + t:qb * TQ + t + 1]
                            last = nc.tensor.matmul(ps_t[:, t * P:(t + 1) * P], col.broadcast_to([P, P]), ident_r[:],
                                                    start=True, stop=True)
                        last.then_inc(tr_full, 1)
                    if step[0] == "out":
                        qb, i = step[1], step[2]
                        pe.wait_ge(ym_free, 1 + sg.ym + NYM * qb + i)
                        if i == 0:
                            pe.wait_ge(y_done, 1 + NQB * sg.main + qb + 1)
                            for t in range(TQ):
                                last = nc.tensor.transpose(ps_y[:, t * P:(t + 1) * P], y_tok[:, qb * TQ + t, :], ident[:])
                        else:
                            if qb == 0:
                                pe.wait_ge(wp_done, 1 + 2 * (sg.pair + 1))
                            for t in range(2):
                                tok = slice((2 * (i - 1) + t) * P, (2 * (i - 1) + t + 1) * P)
                                last = split_product(ps_y[:, t * C:(t + 1) * C], [((yt_hi[:, tok], yt_lo[:, tok]), (wp_hi[:], wp_lo[:]))])
                        last.then_inc(ym_full, 1)

            over_heads(pe, begin, segment, lambda batch: None)



NTOK = 512
NBLK = B * T // NTOK
OC = HID // P
NT = NTOK // P
STAGES = 4
AR = 4


def split_sum(nc, out, pairs):
    terms = [(a, c) for (ah, al), (ch, cl) in pairs for a, c in ((ah, ch), (ah, cl), (al, ch))]
    for i, (a, c) in enumerate(terms):
        last = nc.tensor.matmul(out, a, c, start=i == 0, stop=i == len(terms) - 1)
    return last


def stage_target(item, half, table):
    hi, lo, row, narrow = table[item]
    if narrow:
        cut = slice((row + 2 * half) * P, (row + 2 * half + 2) * P)
        return [w[:, :, cut].rearrange("p k (o c) -> p o k c", o=2) for w in (hi, lo)]
    return [w[:, 4 * half:4 * half + 4, row * P:(row + 1) * P] for w in (hi, lo)]


def ffn_up(nc, sum_dram, x1_dram, w1_w, w1_s, w2_w, w2_s, h1_w, h1_s, a_dram):
    ctx = ExitStack()
    with ctx:
        def sb(name, shape, dt=F32):
            return ctx.enter_context(nc.sbuf_tensor(name, shape, dt))

        def pb(name):
            return ctx.enter_context(nc.psum_tensor(name, [P, 512], F32))

        def sem(name):
            return ctx.enter_context(nc.semaphore(name))

        ident = sb("up_ident", [P, P])
        stage = [sb(f"up_stage{i}", [P, 8 * P]) for i in range(STAGES)]
        w1_hi, w1_lo = sb("w1_hi", [P, KC, HID], F32R), sb("w1_lo", [P, KC, HID], F32R)
        w2_hi, w2_lo = sb("w2_hi", [P, KC, HID], F32R), sb("w2_lo", [P, KC, HID], F32R)
        h1_hi, h1_lo = sb("h1_hi", [P, OC, HID], F32R), sb("h1_lo", [P, OC, HID], F32R)
        scale = sb("up_scale", [P, 3, OC])
        x_tok = sb("x_tok", [P, NT, C])
        stats = sb("up_stats", [P, NT, 6])
        mean_var = sb("up_mean_var", [P, NT, 2])
        rs = sb("up_rs", [P, 2, NT])
        power = sb("up_power", [P, NT])
        x_hi, x_lo = sb("x_hi", [P, KC, NTOK], F32R), sb("x_lo", [P, KC, NTOK], F32R)
        silu = sb("silu", [P, 2, NTOK])
        prod = sb("prod", [P, 2, NTOK])
        p_hi, p_lo = sb("p_hi", [P, OC, NTOK], F32R), sb("p_lo", [P, OC, NTOK], F32R)
        gelu = sb("gelu", [P, AR, NTOK])

        ps_t = [pb(f"up_t{i}") for i in range(2)]
        ps_1 = [pb(f"up_1{i}") for i in range(2)]
        ps_2 = [pb(f"up_2{i}") for i in range(2)]
        ps_h = [pb(f"up_h{i}") for i in range(2)]

        par = sem("up_par")
        made = sem("up_made")
        staged = [sem(f"up_staged{i}") for i in range(STAGES)]
        wt_full = sem("up_wt_full")
        wt_hi = sem("up_wt_hi")
        wt_free = sem("up_wt_free")
        x_load = sem("up_x_load")
        bn_done = sem("up_bn_done")
        var_done = sem("up_var_done")
        rs_done = sem("up_rs_done")
        ln_done = sem("up_ln_done")
        x1_out = sem("up_x1_out")
        xt_full = sem("up_xt_full")
        xt_hi = sem("up_xt_hi")
        xt_free = sem("up_xt_free")
        l1_full = sem("up_l1_full")
        silu_done = sem("up_silu_done")
        l1_free = sem("up_l1_free")
        hi_done = sem("up_hi_done")
        lo_done = sem("up_lo_done")
        l2_full = sem("up_l2_full")
        gelu_done = sem("up_gelu_done")
        stored = [sem(f"up_stored{i}") for i in range(AR)]

        table = [(w1_hi, w1_lo, 4 * i, True) for i in range(2)] + [(w2_hi, w2_lo, 4 * i, True) for i in range(2)] \
            + [(h1_hi, h1_lo, i, False) for i in range(OC)]
        rows = [(w, slice(4 * i * P, 4 * (i + 1) * P)) for w in (w1_w, w2_w) for i in range(2)] \
            + [(h1_w, slice(i * P, (i + 1) * P)) for i in range(OC)]
        NW = 2 * len(table)
        FIRST = 8
        assert NW == FIRST + 2 * OC

        def over_blocks(eng, first_x, body):
            first_x(0)
            body(0, True, True)
            with eng.Fori(1, NBLK - 1) as i:
                body(i, True, False)
            body(NBLK - 1, False, False)

        block = ctx.enter_context(nc.Block())

        def load_x(sp, i):
            rows = sum_dram[bass.ds(i * NTOK, NTOK), :].rearrange("(t p) c -> p t c", p=P)
            if not isinstance(i, int) or i > 0:
                sp.wait_ge(x1_out, 16 * i)
            sp.dma_start(x_tok[:], rows).then_inc(x_load, 16)

        def store_x1(sp, i):
            rows = x1_dram[bass.ds(i * NTOK, NTOK), :].rearrange("(t p) c -> p t c", p=P)
            sp.wait_ge(xt_full, 2 * (i + 1))
            sp.dma_start(rows, x_tok[:]).then_inc(x1_out, 16)

        def sp_body(i, more, first):
            sp = nc.sync
            if more:
                load_x(sp, i + 1)
            for o in range(OC):
                if more and o == 3:
                    store_x1(sp, i + 1)
                sp.wait_ge(gelu_done, 2 + OC * i + o + 1)
                sp.dma_start(a_dram[o * P:(o + 1) * P, bass.ds(i * NTOK, NTOK)], gelu[:, o % AR, :]).then_inc(stored[o % AR], 16)

        @block.sync
        def _(sp):
            load_x(sp, 0)
            for i, s in enumerate((w1_s, w2_s, h1_s)):
                sp.dma_start(scale[:, i, :], s.rearrange("(o p) -> p o", p=P), allow_slow_non_contiguous=True).then_inc(par, 16)
            for i, (w, cut) in enumerate(rows):
                if i >= STAGES:
                    sp.wait_ge(wt_full, 2 * (i - STAGES + 1))
                sp.dma_start(stage[i % STAGES][:].rearrange("p (r c) -> p r c", c=w.shape[1]),
                             w[cut, :].rearrange("(r p) c -> p r c", p=P)).then_inc(staged[i % STAGES], 16)
            over_blocks(sp, lambda i: store_x1(sp, i), sp_body)
            sp.wait_ge(x1_out, 16 * NBLK)
            for s in stored:
                sp.wait_ge(s, 1 + 16 * (OC // AR) * NBLK)

        @block.gpsimd
        def _(gp):
            nc.gpsimd.memset(ident[:], 0.0).then_inc(made, 1)
            gp.wait_ge(made, 1)
            nc.gpsimd.affine_select(out=ident[:], in_=ident[:], compare_op=ALU.not_equal, fill=1.0, base=0,
                                    pattern=[[-1, P]], channel_multiplier=1).then_inc(made, 1)
            nc.gpsimd.memset(power[:], -0.5).then_inc(made, 1)
            gp.wait_ge(made, 3)

            def root(i):
                gp.wait_ge(var_done, i + 1)
                nc.gpsimd.tensor_tensor(rs[:, 1, :], rs[:, 0, :], power[:], ALU.pow).then_inc(rs_done, 1)

            def body(i, more, first):
                if more:
                    root(i + 1)

            over_blocks(gp, root, body)

        @block.scalar
        def _(act):
            act.sem_inc(gelu_done, 2)
            for s in stored:
                act.sem_inc(s, 1)

            def weights(r):
                act.wait_ge(wt_full, r + 1)
                out = stage_target(r // 2, r % 2, table)[0]
                src = ps_t[r % 2][:].rearrange("p (o k c) -> p o k c", o=2, k=2) if table[r // 2][3] \
                    else ps_t[r % 2][:].rearrange("p (k c) -> p k c", k=4)
                nc.scalar.activation(out, src, ACT.Copy).then_inc(wt_hi, 1)

            for r in range(FIRST):
                weights(r)

            def turn_x(i):
                for e in range(2):
                    act.wait_ge(xt_full, 2 * i + e + 1)
                    nc.scalar.activation(x_hi[:, :, 2 * e * P:2 * (e + 1) * P],
                                         ps_t[e][:].rearrange("p (k t) -> p k t", k=KC), ACT.Copy).then_inc(xt_hi, 1)

            def body(i, more, first):
                for o in range(OC):
                    if first:
                        weights(FIRST + 2 * o)
                        weights(FIRST + 2 * o + 1)
                    act.wait_ge(l1_full, OC * i + o + 1)
                    if o == 0:
                        act.wait_ge(par, 48)
                    nc.scalar.activation(silu[:, o % 2, :], ps_1[o % 2][:], ACT.Silu, scale=scale[:, 0, o:o + 1]).then_inc(silu_done, 1)
                    act.wait_ge(l1_free, 2 + OC * i + o + 1)
                    nc.scalar.activation(p_hi[:, o, :], prod[:, o % 2, :], ACT.Copy).then_inc(hi_done, 1)
                for o in range(OC):
                    if o == 3 and more:
                        turn_x(i + 1)
                    act.wait_ge(l2_full, OC * i + o + 1)
                    act.wait_ge(stored[o % AR], 1 + 16 * ((OC // AR) * i + o // AR))
                    nc.scalar.activation(gelu[:, o % AR, :], ps_h[o % 2][:], ACT.Gelu, scale=scale[:, 2, o:o + 1]).then_inc(gelu_done, 1)
                if more:
                    nc.scalar.preload_act_table(ACT.Silu)

            over_blocks(act, turn_x, body)

        @block.vector
        def _(dve):
            dve.sem_inc(xt_free, 2)
            dve.sem_inc(l1_free, 2)
            dve.sem_inc(lo_done, 2)

            def weights(r):
                dve.wait_ge(wt_hi, r + 1)
                hi, lo = stage_target(r // 2, r % 2, table)
                src = ps_t[r % 2][:].rearrange("p (o k c) -> p o k c", o=2, k=2) if table[r // 2][3] \
                    else ps_t[r % 2][:].rearrange("p (k c) -> p k c", k=4)
                nc.vector.tensor_tensor(lo, src, hi.bitcast(F32), ALU.subtract).then_inc(wt_free, 1)

            def normalise_x(i):
                dve.wait_ge(x_load, 16 * (i + 1))
                for t in range(NT):
                    last = nc.vector.bn_stats(stats[:, t, :], x_tok[:, t, :])
                last.then_inc(bn_done, 1)
                dve.wait_ge(bn_done, 2 * i + 1)
                nc.vector.memset(rs[:, 0, :], 1.0)
                for t in range(NT):
                    last = nc.vector.bn_aggr(mean_var[:, t, :], stats[:, t, :])
                last.then_inc(bn_done, 1)
                dve.wait_ge(bn_done, 2 * i + 2)
                nc.vector.tensor_scalar(rs[:, 0, :], mean_var[:, :, 1], EPS_LN, None, ALU.add).then_inc(var_done, 1)
                dve.wait_ge(rs_done, i + 1)
                for t in range(NT):
                    last = nc.vector.tensor_scalar(x_tok[:, t, :], x_tok[:, t, :], mean_var[:, t, 0:1], rs[:, 1, t:t + 1],
                                                   ALU.subtract, ALU.mult)
                last.then_inc(ln_done, 1)

            normalise_x(0)
            for r in range(FIRST):
                weights(r)
            dve.wait_ge(par, 48)

            def turn_x(i):
                for e in range(2):
                    dve.wait_ge(xt_hi, 2 * i + e + 1)
                    cut = slice(2 * e * P, 2 * (e + 1) * P)
                    nc.vector.tensor_tensor(x_lo[:, :, cut], ps_t[e][:].rearrange("p (k t) -> p k t", k=KC),
                                            x_hi[:, :, cut].bitcast(F32), ALU.subtract).then_inc(xt_free, 1)

            def body(i, more, first):
                for o in range(OC):
                    if first:
                        weights(FIRST + 2 * o)
                        weights(FIRST + 2 * o + 1)
                    dve.wait_ge(silu_done, OC * i + o + 1)
                    dve.wait_ge(lo_done, 2 + OC * i + o - 1)
                    nc.vector.scalar_tensor_tensor(prod[:, o % 2, :], ps_2[o % 2][:], scale[:, 1, o:o + 1], silu[:, o % 2, :],
                                                   ALU.mult, ALU.mult).then_inc(l1_free, 1)
                    dve.wait_ge(hi_done, OC * i + o + 1)
                    nc.vector.tensor_tensor(p_lo[:, o, :], prod[:, o % 2, :], p_hi[:, o, :].bitcast(F32), ALU.subtract).then_inc(lo_done, 1)
                if more:
                    normalise_x(i + 1)
                    turn_x(i + 1)

            over_blocks(dve, turn_x, body)

        @block.tensor
        def _(pe):
            pe.wait_ge(made, 2)

            def weights(r):
                pe.wait_ge(staged[(r // 2) % STAGES], 16 * (r // 2 // STAGES + 1))
                if r >= 2:
                    pe.wait_ge(wt_free, r - 1)
                for q in range(4):
                    last = nc.tensor.transpose(ps_t[r % 2][:, q * P:(q + 1) * P],
                                               stage[(r // 2) % STAGES][:, (4 * (r % 2) + q) * P:(4 * (r % 2) + q + 1) * P], ident[:])
                last.then_inc(wt_full, 1)

            for r in range(FIRST):
                weights(r)
            pe.wait_ge(wt_free, FIRST)

            def turn_x(i):
                pe.wait_ge(ln_done, i + 1)
                for e in range(2):
                    pe.wait_ge(xt_free, 2 * i + e + 1)
                    for k in range(KC):
                        for t in range(2):
                            last = nc.tensor.transpose(ps_t[e][:, (2 * k + t) * P:(2 * k + t + 1) * P],
                                                       x_tok[:, 2 * e + t, k * P:(k + 1) * P], ident[:])
                    last.then_inc(xt_full, 1)

            def body(i, more, first):
                for o in range(OC):
                    col = slice(o * P, (o + 1) * P)
                    if o == 0:
                        pe.wait_ge(xt_free, 2 + 2 * (i + 1))
                    if first:
                        weights(FIRST + 2 * o)
                        weights(FIRST + 2 * o + 1)
                    pe.wait_ge(l1_free, 2 + OC * i + o - 1)
                    split_sum(nc, ps_1[o % 2][:], [((w1_hi[:, k, col], w1_lo[:, k, col]), (x_hi[:, k, :], x_lo[:, k, :])) for k in range(KC)])
                    split_sum(nc, ps_2[o % 2][:], [((w2_hi[:, k, col], w2_lo[:, k, col]), (x_hi[:, k, :], x_lo[:, k, :]))
                                                   for k in range(KC)]).then_inc(l1_full, 1)
                if first:
                    pe.wait_ge(wt_free, NW)
                for o in range(OC):
                    col = slice(o * P, (o + 1) * P)
                    if o == 3 and more:
                        turn_x(i + 1)
                    pe.wait_ge(gelu_done, 2 + OC * i + o - 1)
                    for k in range(OC):
                        if o == 0:
                            pe.wait_ge(lo_done, 2 + OC * i + k + 1)
                        for j, (w, p) in enumerate(((h1_hi, p_hi), (h1_lo, p_hi), (h1_hi, p_lo))):
                            last = nc.tensor.matmul(ps_h[o % 2][:], w[:, k, col], p[:, k, :], start=k == 0 and j == 0,
                                                    stop=k == OC - 1 and j == 2)
                    last.then_inc(l2_full, 1)

            over_blocks(pe, turn_x, body)


def ffn_down(nc, a_dram, x1_dram, h2_w, h2_s, w3_w, w3_s, out):
    ctx = ExitStack()
    with ctx:
        def sb(name, shape, dt=F32):
            return ctx.enter_context(nc.sbuf_tensor(name, shape, dt))

        def pb(name):
            return ctx.enter_context(nc.psum_tensor(name, [P, 512], F32))

        def sem(name):
            return ctx.enter_context(nc.semaphore(name))

        ident = sb("dn_ident", [P, P])
        stage = [sb(f"dn_stage{i}", [P, 8 * P]) for i in range(2)]
        h2_hi, h2_lo = sb("h2_hi", [P, OC, HID], F32R), sb("h2_lo", [P, OC, HID], F32R)
        w3_hi, w3_lo = sb("w3_hi", [P, OC, C], F32R), sb("w3_lo", [P, OC, C], F32R)
        scale = sb("dn_scale", [P, OC])
        scale_out = sb("dn_scale_out", [P, C])
        a_in = sb("a_in", [P, OC, NTOK])
        a_hi, a_lo = sb("a_hi", [P, OC, NTOK], F32R), sb("a_lo", [P, OC, NTOK], F32R)
        gelu = sb("dn_gelu", [P, 2, NTOK])
        b_hi, b_lo = sb("b_hi", [P, OC, NTOK], F32R), sb("b_lo", [P, OC, NTOK], F32R)
        x_tok = sb("dn_x", [P, NT, C])
        y = sb("dn_y", [P, NT, C])
        stats = sb("dn_stats", [P, NT, 6])
        mean_var = sb("dn_mean_var", [P, NT, 2])
        rs = sb("dn_rs", [P, 2, NT])
        power = sb("dn_power", [P, NT])

        ps_t = [pb(f"dn_t{i}") for i in range(2)]
        ps_h = [pb(f"dn_h{i}") for i in range(2)]
        ps_o = [pb(f"dn_o{i}") for i in range(2)]

        par = sem("dn_par")
        made = sem("dn_made")
        staged = [sem(f"dn_staged{i}") for i in range(2)]
        wt_full = sem("dn_wt_full")
        wt_hi = sem("dn_wt_hi")
        wt_free = sem("dn_wt_free")
        a_load = sem("dn_a_load")
        x_load = sem("dn_x_load")
        ahi_done = sem("dn_ahi_done")
        alo_done = sem("dn_alo_done")
        l3_full = sem("dn_l3_full")
        gelu_done = sem("dn_gelu_done")
        bhi_done = sem("dn_bhi_done")
        blo_done = sem("dn_blo_done")
        l4_full = sem("dn_l4_full")
        l4_free = sem("dn_l4_free")
        sum_done = sem("dn_sum_done")
        bn_done = sem("dn_bn_done")
        var_done = sem("dn_var_done")
        rs_done = sem("dn_rs_done")
        ln_done = sem("dn_ln_done")
        out_done = sem("dn_out_done")

        table = [(h2_hi, h2_lo, i, False) for i in range(OC)] + [(w3_hi, w3_lo, i, False) for i in range(KC)]
        rows = [(h2_w, slice(i * P, (i + 1) * P)) for i in range(OC)] + [(w3_w, slice(i * P, (i + 1) * P)) for i in range(KC)]
        NW = 2 * len(table)

        def over_blocks(eng, split_a, body):
            split_a(0)
            body(0, True, True)
            with eng.Fori(1, NBLK - 1) as i:
                body(i, True, False)
            body(NBLK - 1, False, False)

        def weights_at(o):
            return range(2 * (o + 1), NW if o == OC - 1 else 2 * (o + 2))

        block = ctx.enter_context(nc.Block())

        def load_a(sp, i):
            sp.dma_start(a_in[:], a_dram[:, bass.ds(i * NTOK, NTOK)].rearrange("(k p) n -> p k n", p=P)).then_inc(a_load, 16)

        def sp_body(i, more, first):
            sp = nc.sync
            sp.wait_ge(sum_done, 1 + NT * i)
            sp.dma_start(x_tok[:], x1_dram[bass.ds(i * NTOK, NTOK), :].rearrange("(t p) c -> p t c", p=P)).then_inc(x_load, 16)
            if more:
                sp.wait_ge(alo_done, 1 + OC * (i + 1))
                load_a(sp, i + 1)
            sp.wait_ge(ln_done, i + 1)
            sp.dma_start(out[bass.ds(i * NTOK, NTOK), :].rearrange("(t p) c -> p t c", p=P), y[:]).then_inc(out_done, 16)

        @block.sync
        def _(sp):
            sp.dma_start(scale[:], h2_s.rearrange("(o p) -> p o", p=P), allow_slow_non_contiguous=True).then_inc(par, 16)
            sp.dma_start(scale_out[:], w3_s.partition_broadcast(P)).then_inc(par, 16)
            for i, (w, cut) in enumerate(rows):
                if i >= 2:
                    sp.wait_ge(wt_full, 2 * (i - 1))
                sp.dma_start(stage[i % 2][:], w[cut, :]).then_inc(staged[i % 2], 16)
                if i == 1:
                    load_a(sp, 0)
            over_blocks(sp, lambda i: None, sp_body)
            sp.wait_ge(out_done, 1 + 16 * NBLK)

        @block.gpsimd
        def _(gp):
            nc.gpsimd.memset(power[:], -0.5)
            nc.gpsimd.memset(ident[:], 0.0).then_inc(made, 1)
            gp.wait_ge(made, 1)
            nc.gpsimd.affine_select(out=ident[:], in_=ident[:], compare_op=ALU.not_equal, fill=1.0, base=0,
                                    pattern=[[-1, P]], channel_multiplier=1).then_inc(made, 1)

            def body(i, more, first):
                gp.wait_ge(var_done, i + 1)
                nc.gpsimd.tensor_tensor(rs[:, 1, :], rs[:, 0, :], power[:], ALU.pow).then_inc(rs_done, 1)

            over_blocks(gp, lambda i: None, body)

        @block.scalar
        def _(act):
            act.sem_inc(gelu_done, 2)
            nc.scalar.preload_act_table(ACT.Gelu)

            def weights(r):
                act.wait_ge(wt_full, r + 1)
                nc.scalar.activation(stage_target(r // 2, r % 2, table)[0], ps_t[r % 2][:].rearrange("p (k c) -> p k c", k=4),
                                     ACT.Copy).then_inc(wt_hi, 1)

            for r in range(2):
                weights(r)
            act.wait_ge(par, 32)

            def split_a(i):
                act.wait_ge(a_load, 16 * (i + 1))
                for k in range(OC):
                    if k == 0:
                        act.wait_ge(l3_full, 1 + OC * i)
                    nc.scalar.activation(a_hi[:, k, :], a_in[:, k, :], ACT.Copy).then_inc(ahi_done, 1)

            def body(i, more, first):
                for o in range(OC):
                    for r in weights_at(o) if first else ():
                        weights(r)
                    act.wait_ge(l3_full, 1 + OC * i + o + 1)
                    act.wait_ge(blo_done, 2 + OC * i + o - 1)
                    nc.scalar.activation(gelu[:, o % 2, :], ps_h[o % 2][:], ACT.Gelu, scale=scale[:, o:o + 1]).then_inc(gelu_done, 1)
                    act.wait_ge(gelu_done, 2 + OC * i + o + 1)
                    if o == 0:
                        act.wait_ge(l4_full, 1 + NT * i)
                    nc.scalar.activation(b_hi[:, o, :], gelu[:, o % 2, :], ACT.Copy).then_inc(bhi_done, 1)
                if more:
                    split_a(i + 1)

            over_blocks(act, split_a, body)

        @block.vector
        def _(dve):
            dve.sem_inc(alo_done, 1)
            dve.sem_inc(blo_done, 2)
            dve.sem_inc(l4_free, 2)
            dve.sem_inc(sum_done, 1)
            dve.sem_inc(out_done, 1)

            def weights(r):
                dve.wait_ge(wt_hi, r + 1)
                hi, lo = stage_target(r // 2, r % 2, table)
                nc.vector.tensor_tensor(lo, ps_t[r % 2][:].rearrange("p (k c) -> p k c", k=4), hi.bitcast(F32),
                                        ALU.subtract).then_inc(wt_free, 1)

            for r in range(2):
                weights(r)
            dve.wait_ge(par, 32)

            def split_a(i, tiles=range(OC)):
                for k in tiles:
                    dve.wait_ge(ahi_done, OC * i + k + 1)
                    nc.vector.tensor_tensor(a_lo[:, k, :], a_in[:, k, :], a_hi[:, k, :].bitcast(F32), ALU.subtract).then_inc(alo_done, 1)

            def body(i, more, first):
                for o in range(OC):
                    for r in weights_at(o) if first else ():
                        weights(r)
                    dve.wait_ge(bhi_done, OC * i + o + 1)
                    nc.vector.tensor_tensor(b_lo[:, o, :], gelu[:, o % 2, :], b_hi[:, o, :].bitcast(F32), ALU.subtract).then_inc(blo_done, 1)
                if more:
                    split_a(i + 1, range(OC // 4))
                dve.wait_ge(x_load, 16 * (i + 1))
                dve.wait_ge(out_done, 1 + 16 * i)
                for t in range(NT):
                    if more and t > 0:
                        split_a(i + 1, range(t * OC // 4, (t + 1) * OC // 4))
                    dve.wait_ge(l4_full, 1 + NT * i + t + 1)
                    nc.vector.tensor_tensor(y[:, t, :], ps_o[t % 2][:, 0:C], scale_out[:], ALU.mult).then_inc(l4_free, 1)
                    dve.wait_ge(l4_free, 2 + NT * i + t + 1)
                    nc.vector.tensor_tensor(y[:, t, :], y[:, t, :], x_tok[:, t, :], ALU.add).then_inc(sum_done, 1)
                dve.wait_ge(sum_done, 1 + NT * (i + 1))
                for t in range(NT):
                    last = nc.vector.bn_stats(stats[:, t, :], y[:, t, :])
                last.then_inc(bn_done, 1)
                dve.wait_ge(bn_done, 2 * i + 1)
                nc.vector.memset(rs[:, 0, :], 1.0)
                for t in range(NT):
                    last = nc.vector.bn_aggr(mean_var[:, t, :], stats[:, t, :])
                last.then_inc(bn_done, 1)
                dve.wait_ge(bn_done, 2 * i + 2)
                nc.vector.tensor_scalar(rs[:, 0, :], mean_var[:, :, 1], EPS_LN, None, ALU.add).then_inc(var_done, 1)
                dve.wait_ge(rs_done, i + 1)
                for t in range(NT):
                    last = nc.vector.tensor_scalar(y[:, t, :], y[:, t, :], mean_var[:, t, 0:1], rs[:, 1, t:t + 1],
                                                   ALU.subtract, ALU.mult)
                last.then_inc(ln_done, 1)

            over_blocks(dve, split_a, body)

        @block.tensor
        def _(pe):
            pe.wait_ge(made, 2)
            pe.sem_inc(l3_full, 1)
            pe.sem_inc(l4_full, 1)

            def weights(r):
                pe.wait_ge(staged[(r // 2) % 2], 16 * (r // 4 + 1))
                if r >= 2:
                    pe.wait_ge(wt_free, r - 1)
                for q in range(4):
                    last = nc.tensor.transpose(ps_t[r % 2][:, q * P:(q + 1) * P],
                                               stage[(r // 2) % 2][:, (4 * (r % 2) + q) * P:(4 * (r % 2) + q + 1) * P], ident[:])
                last.then_inc(wt_full, 1)

            for r in range(2):
                weights(r)

            def body(i, more, first):
                for o in range(OC):
                    col = slice(o * P, (o + 1) * P)
                    if first:
                        for r in weights_at(o):
                            weights(r)
                        pe.wait_ge(wt_free, 2 * (o + 1))
                    pe.wait_ge(gelu_done, 2 + OC * i + o - 1)
                    for k in range(OC):
                        if o == 0:
                            pe.wait_ge(alo_done, 1 + OC * i + k + 1)
                        for j, (w, p) in enumerate(((h2_hi, a_hi), (h2_lo, a_hi), (h2_hi, a_lo))):
                            last = nc.tensor.matmul(ps_h[o % 2][:], w[:, k, col], p[:, k, :], start=k == 0 and j == 0,
                                                    stop=k == OC - 1 and j == 2)
                    last.then_inc(l3_full, 1)
                if first:
                    pe.wait_ge(wt_free, NW)
                for t in range(NT):
                    tok = slice(t * P, (t + 1) * P)
                    pe.wait_ge(l4_free, 2 + NT * i + t - 1)
                    for k in range(OC):
                        if t == 0:
                            pe.wait_ge(blo_done, 2 + OC * i + k + 1)
                        for j, (p, w) in enumerate(((b_hi, w3_hi), (b_hi, w3_lo), (b_lo, w3_hi))):
                            last = nc.tensor.matmul(ps_o[t % 2][:, 0:C], p[:, k, tok], w[:, k, :], start=k == 0 and j == 0,
                                                    stop=k == OC - 1 and j == 2)
                    last.then_inc(l4_full, 1)

            over_blocks(pe, lambda i: None, body)


def program(nc, a, out):
    attended = nc.dram_tensor("attended", (B * T, C), F32, kind="Internal").ap()
    x1 = nc.dram_tensor("x1", (B * T, C), F32, kind="Internal").ap()
    hidden = nc.dram_tensor("hidden", (HID, B * T), F32, kind="Internal").ap()
    attention(nc, a["L0_attn_x"], a["L0_attn_Wq"], a["L0_attn_Wk"], a["L0_attn_Wv"], a["L0_attn_Wproj"],
              a["L0_attn_q_rms_w"], a["L0_attn_k_rms_w"], a["L0_attn_omega"], a["L0_attn_u"], attended)
    ffn_up(nc, attended, x1, a["L0_ffn_w1_w"], a["L0_ffn_w1_s"], a["L0_ffn_w2_w"], a["L0_ffn_w2_s"], a["L0_ffn_h1_w"],
           a["L0_ffn_h1_s"], hidden)
    ffn_down(nc, hidden, x1, a["L0_ffn_h2_w"], a["L0_ffn_h2_s"], a["L0_ffn_w3_w"], a["L0_ffn_w3_s"], out)


SHAPES = {"L0_attn_x": (B * T, C), "L0_attn_Wq": (C, H * D), "L0_attn_Wk": (C, H * D), "L0_attn_Wv": (C, H * D),
          "L0_attn_Wproj": (H * D, C), "L0_attn_q_rms_w": (D,), "L0_attn_k_rms_w": (D,), "L0_attn_omega": (H,),
          "L0_attn_u": (H, D), "L0_ffn_w1_w": (HID, C), "L0_ffn_w1_s": (HID,), "L0_ffn_w2_w": (HID, C),
          "L0_ffn_w2_s": (HID,), "L0_ffn_h1_w": (HID, HID), "L0_ffn_h1_s": (HID,), "L0_ffn_h2_w": (HID, HID),
          "L0_ffn_h2_s": (HID,), "L0_ffn_w3_w": (C, HID), "L0_ffn_w3_s": (C,)}


def kernel(**inputs):
    import numpy as _np
    import concourse.bacc as _bacc
    from concourse import mybir as _mybir
    from concourse.bass_utils import run_bass_kernel_spmd as _run

    nc = _bacc.Bacc("TRN2", target_bir_lowering=False, num_devices=1)
    arrays, aps = {}, {}
    for name, shape in SHAPES.items():
        a = _np.ascontiguousarray(inputs[name]).reshape(shape)
        arrays[f"in_{name}_dram"] = a
        aps[name] = nc.dram_tensor(f"in_{name}_dram", a.shape, _mybir.dt.from_np(a.dtype), kind="ExternalInput").ap()
    out = nc.dram_tensor("out_0_dram", (B * T, C), _mybir.dt.float32, kind="ExternalOutput").ap()
    program(nc, aps, out)
    r = _run(nc, [arrays], core_ids=[0])
    return r.results[0]["out_0_dram"].reshape(B, T, C)
```
